# Optimizing a Trainium2 kernel written in Bass

```python
import numpy as np
import jax
import jax.numpy as jnp

def _softmax(x, axis=-1):
    return jax.nn.softmax(x, axis=axis)

def _gelu(x):
    return jax.nn.gelu(x, approximate=True)

def _silu(x):
    return jax.nn.silu(x)

def _sigmoid(x):
    return jax.nn.sigmoid(x)

def _layernorm(x, axis=-1, eps=1e-05):
    m = jnp.mean(x, axis=axis, keepdims=True)
    v = jnp.var(x, axis=axis, keepdims=True)
    return (x - m) / jnp.sqrt(v + eps)

def _scatter_add(tgt, idx, src, axis=0):
    return tgt.at[idx].add(src)

def _segment_sum(src, seg, n):
    return jax.ops.segment_sum(src, seg, n)
kernel_name = 'mk_gnn_resnorm_d1_gnn_r64_88dbed'

def setup_inputs(seed: int=0):
    np.random.seed(seed)
    _w = jnp.asarray

    def _rec_inputs():
        import jax
        import jax.numpy as jnp
        _gk = jax.random.key(seed)
        x = -0.0003713 + 1 * jax.random.normal(jax.random.fold_in(_gk, 1), (100000, 256), jnp.float32)
        src = jax.random.randint(jax.random.fold_in(_gk, 2), (25000,), 0, 100000, jnp.int32)
        dst = jnp.minimum((100000 * jax.random.uniform(jax.random.fold_in(_gk, 3), (25000,)) ** 2.0).astype(jnp.int32), 99999)
        _o = jnp.argsort(dst, stable=True)
        src = src[_o]
        dst = dst[_o]
        edge_type_16 = jax.random.randint(jax.random.fold_in(_gk, 12), (25000,), 0, 16, jnp.int32)
        return (x, src, dst, edge_type_16)
    x, src, dst, edge_type_16 = _rec_inputs()

    def _L0_gnn_setup():
        import jax, jax.numpy as jnp
        import numpy as np
        NUM_BLOCKS = 64

        def rgcn_layer(x, src, dst, edge_type, W, root, bias):
            N, d = x.shape
            xj = x[src]
            out0 = x @ root + bias

            def body(out, inputs):
                r, Wr = inputs
                mask = (edge_type == r).astype(x.dtype)
                s = jax.ops.segment_sum(xj * mask[:, None], dst, num_segments=N)
                cnt = jax.ops.segment_sum(mask, dst, num_segments=N)
                h = s / jnp.maximum(cnt, 1.0)[:, None]
                hb = h.reshape(N, NUM_BLOCKS, d // NUM_BLOCKS)
                out = out + jnp.einsum('nbi,bio->nbo', hb, Wr).reshape(N, d)
                return (out, None)
            R = W.shape[0]
            out, _ = jax.lax.scan(body, out0, (jnp.arange(R), W))
            return out
        key = jax.random.key(seed)
        ks = jax.random.split(key, 9)
        N, d, R, E = (50000, 256, 16, 12500)
        db = d // NUM_BLOCKS
        return {'node_emb': jax.random.normal(ks[0], (N, d), jnp.float32), 'edge_index': jax.random.randint(ks[1], (2, E), 0, N), 'edge_type': jax.random.randint(ks[2], (E,), 0, R), 'W1': jax.random.normal(ks[3], (R, NUM_BLOCKS, db, db), jnp.float32) * 0.1, 'root1': jax.random.normal(ks[4], (d, d), jnp.float32) * 0.05, 'bias1': jnp.zeros((d,), jnp.float32), 'W2': jax.random.normal(ks[5], (R, NUM_BLOCKS, db, db), jnp.float32) * 0.1, 'root2': jax.random.normal(ks[6], (d, d), jnp.float32) * 0.05, 'bias2': jnp.zeros((d,), jnp.float32)}
    _L0_gnn_all = _L0_gnn_setup()
    _L0_gnn_in = {k: v for k, v in _L0_gnn_all.items() if k in ('W1', 'root1', 'bias1', 'W2', 'root2', 'bias2')}
    del _L0_gnn_all
    return {'x': x, 'src': src, 'dst': dst, 'edge_type_16': edge_type_16, 'L0_gnn_W1': _L0_gnn_in['W1'], 'L0_gnn_root1': _L0_gnn_in['root1'], 'L0_gnn_bias1': _L0_gnn_in['bias1'], 'L0_gnn_W2': _L0_gnn_in['W2'], 'L0_gnn_root2': _L0_gnn_in['root2'], 'L0_gnn_bias2': _L0_gnn_in['bias2']}

def reference(x, src, dst, edge_type_16, L0_gnn_W1, L0_gnn_root1, L0_gnn_bias1, L0_gnn_W2, L0_gnn_root2, L0_gnn_bias2):
    import jax
    import jax.numpy as jnp

    def _L0_gnn_ref(node_emb, edge_index, edge_type, W1, root1, bias1, W2, root2, bias2):
        import jax, jax.numpy as jnp
        import numpy as np
        NUM_BLOCKS = 64

        def rgcn_layer(x, src, dst, edge_type, W, root, bias):
            N, d = x.shape
            xj = x[src]
            out0 = x @ root + bias

            def body(out, inputs):
                r, Wr = inputs
                mask = (edge_type == r).astype(x.dtype)
                s = jax.ops.segment_sum(xj * mask[:, None], dst, num_segments=N)
                cnt = jax.ops.segment_sum(mask, dst, num_segments=N)
                h = s / jnp.maximum(cnt, 1.0)[:, None]
                hb = h.reshape(N, NUM_BLOCKS, d // NUM_BLOCKS)
                out = out + jnp.einsum('nbi,bio->nbo', hb, Wr).reshape(N, d)
                return (out, None)
            R = W.shape[0]
            out, _ = jax.lax.scan(body, out0, (jnp.arange(R), W))
            return out
        src, dst = (edge_index[0], edge_index[1])
        x = jax.nn.relu(rgcn_layer(node_emb, src, dst, edge_type, W1, root1, bias1))
        x = rgcn_layer(x, src, dst, edge_type, W2, root2, bias2)
        return x
    edge_index = jnp.stack([src, dst])
    x = _layernorm(x + _L0_gnn_ref(x, edge_index, edge_type_16, L0_gnn_W1, L0_gnn_root1, L0_gnn_bias1, L0_gnn_W2, L0_gnn_root2, L0_gnn_bias2), axis=-1)
    return x

_drawn_inputs = setup_inputs


def setup_inputs(seed=0):
    import zlib

    import numpy as np

    out = dict(_drawn_inputs(seed))
    spreads = {'L0_gnn_bias1': (0.0, 0.1), 'L0_gnn_bias2': (0.0, 0.1)}
    factors = {}
    for name, (base, spread) in spreads.items():
        noise = np.random.default_rng([zlib.crc32(name.encode()), seed]).standard_normal(out[name].shape)
        drawn = base * np.exp(spread * noise) if base else spread * noise
        out[name] = jnp.asarray(drawn.astype(out[name].dtype))
    for name, factor in factors.items():
        out[name] = (out[name] * factor).astype(out[name].dtype)
    return out
```

```python
from contextlib import ExitStack

import concourse.bass as bass
from concourse import mybir
from concourse.alu_op_type import AluOpType as ALU

N, D, E, R = 100000, 256, 25000, 16
P = 128
EC = P - 2
NCH = -(-E // (4 * EC)) * 4
SLOTS = NCH * P
BIG = 1 << 20
SEG = 8
SL = E // SEG
LIN = EC * (NCH + 1)
G = 512
NG = N // G
REM = N - NG * G
RP = REM // 4
PRO = 8
A_IT = (NCH - PRO) // 4
A_G = PRO // 2
B_IT = (NG + 1 - A_G - 2 * A_IT - 4) // 2
C_PRO = 12
C_IT = (NCH - C_PRO) // 4
C_LEAD = 6
B_IT = (NG + 1 - A_G - 2 * A_IT - 4) // 2
B_LEFT = NCH - PRO - 4 * B_IT
EPS = 1e-5
PIECES = -(-SL // 512)
TROW = 1024
TROWS = -(-SLOTS // TROW)
assert C_PRO + 4 * C_IT == NCH
assert PRO + 4 * B_IT + 8 == NCH and A_G + 2 * A_IT + 2 * B_IT + 4 == NG + 1
F32, BF16, I32 = mybir.dt.float32, mybir.dt.bfloat16, mybir.dt.int32
ACT = mybir.ActivationFunctionType
AX = mybir.AxisListType


class Idx:

    def __init__(self, at, i=None, by=4):
        self.at, self.i, self.by = at, i, by
        self.n = at if i is None else i * by + at

    def plus(self, k):
        return Idx(self.at + k, self.i, self.by)

    def times(self, k, more=0):
        return self.at * k + more if self.i is None else self.i * (self.by * k) + (self.at * k + more)

    def used(self, k):
        return self.at // k * 16 if self.i is None else self.i * (self.by // k * 16) + self.at // k * 16

    def inn(self, k):
        return self.at // k * 16 + 16 if self.i is None else self.i * (self.by // k * 16) + (self.at // k * 16 + 16)


def program(nc, x, src, dst, typ, dstseg, typseg, w1, w2, root1, root2, b1, b2, tri, iota, ppos,
            rel, sel, ident, anti, slotid, y):
    ctx = ExitStack()
    with ctx:
        def sb(name, shape, dt=F32):
            return ctx.enter_context(nc.sbuf_tensor(name, shape, dt))

        def sem(name):
            return ctx.enter_context(nc.semaphore(name))

        def sems(name, n):
            return [sem(f"{name}{k}") for k in range(n)]

        seg_ends = nc.dram_tensor("seg_ends", (P, 4), F32).ap()
        seg_carry = nc.dram_tensor("seg_carry", (P, 2), F32).ap()
        lin_inv = nc.dram_tensor("lin_inv", (LIN,), F32).ap()
        lin_len = nc.dram_tensor("lin_len", (LIN,), F32).ap()
        node_slot = nc.dram_tensor("node_slot", (N, 1), I32).ap()
        agg1 = nc.dram_tensor("agg1", (SLOTS, D), F32).ap()
        agg2 = nc.dram_tensor("agg2", (SLOTS, D), F32).ap()

        root1_sb = sb("root1_sb", [P, 2, D])
        root2_sb = sb("root2_sb", [P, 2, D])
        b1_col = sb("b1_col", [P, 2])
        b2_row = sb("b2_row", [3, D])
        b2_res = sb("b2_res", [3, D])
        b2_parts = sb("b2_parts", [3, 3, D], BF16)
        b2_mask = sb("b2_mask", [3, 3])
        b2_sel = sb("b2_sel", [3, D])
        b2_bf = sb("b2_bf", [3, 2, D], BF16)
        ones3 = sb("ones3", [3, P], BF16)
        first_carry = sb("first_carry", [2, 2, D])
        tri_sb = sb("tri_sb", [P, P])
        iota_sb = sb("iota_sb", [P, P])
        ppos_sb = sb("ppos_sb", [P, 1])
        rel_sb = sb("rel_sb", [P, 2])
        sel_sb = sb("sel_sb", [P, SEG])
        ident_sb = sb("ident_sb", [P, P])
        anti_sb = sb("anti_sb", [P, P])
        eps_col = sb("eps_col", [P, 1])
        wcat = sb("wcat", [96, 2, 4 * D], BF16)
        wf = sb("wf", [96, 4 * D])
        src_sb = sb("src_sb", [P, NCH], I32)
        dst_sb = sb("dst_sb", [P, NCH], I32)
        slotid_sb = sb("slotid_sb", [P, NCH], I32)
        onehot = sb("onehot", [96, SLOTS], BF16)
        inv_sb = sb("inv_sb", [P, NCH])
        len_sb = sb("len_sb", [P, NCH])
        start_sb = sb("start_sb", [P, NCH])
        later = sb("later", [P, NCH])
        first_dst = sb("first_dst", [P, NCH], I32)
        trow = sb("trow", [96, TROW], I32)
        ends = sb("ends", [P, 4])
        ends_r = sb("ends_r", [R, SEG, 4])
        carry_r = sb("carry_r", [R, SEG, 2])
        carry = sb("carry", [P, 2])
        ltile = sb("ltile", [P, 4, P])
        fill = sb("fill", [80, N // 80], I32)
        pad_one = sb("pad_one", [1, LIN - E])
        st_d = sb("st_d", [P, 4, 6])
        mv_d = sb("mv_d", [P, 4, 2])
        sd_d, rs_d, nb_d = (sb(s, [P, 4]) for s in ("sd_d", "rs_d", "nb_d"))
        ix = sb("ix", [P, 3, 4], I32)
        slot_ix = sb("slot_ix", [P, 4], I32)
        st_e = sb("st_e", [P, 2, 6])
        mv_e = sb("mv_e", [P, 2, 2])
        sd_e, rs_e, nb_e = (sb(s, [P, 2]) for s in ("sd_e", "rs_e", "nb_e"))

        work = sb("work", [P, 7 * (SL + 2)])

        def carver():
            at = [0]

            def carve(*shape):
                size = 1
                for k in shape:
                    size *= k
                flat = work[:, at[0]:at[0] + size]
                at[0] += size
                assert at[0] <= 7 * (SL + 2)
                if len(shape) == 1:
                    return flat
                if len(shape) == 2:
                    return flat.rearrange("p (a b) -> p a b", a=shape[0])
                return flat.rearrange("p (a b c) -> p a b c", a=shape[0], b=shape[1])
            return carve

        carve = carver()
        dseg, tseg = carve(SL + 2).bitcast(I32), carve(SL).bitcast(I32)
        same, oh, fwd, bwd, cont = carve(SL + 1), carve(SL), carve(SL), carve(SL), carve(SL)
        sums = (cont[0:SEG, :], same[0:SEG, 0:SL])
        carve = carver()
        xg, zg = carve(2, 4, D), carve(2, 4, D)
        xt, ht = carve(2, G), carve(2, G)
        xe, ae = carve(4, D), carve(4, D)
        tri_inv, smat = carve(2, P), carve(2, P)
        xet, hpre, he, het = carve(2, D), carve(2, D), carve(2, D), carve(2, D)
        prod, msg, ao = carve(2, 4 * D), carve(2, D), carve(2, D)
        a1l, a2l, ze, xa = carve(4, D), carve(4, D), carve(4, D), carve(4, D)

        psum = ctx.enter_context(nc.psum_tensor("psum", [P, 8, 512], F32))
        XT, AG, HT, ZB, WG, EB = 0, 1, (2, 3), 4, 5, 7
        CT1, CM1, CT2, CM2 = (0, 1), (2, 3), (4, 7), (5, 6)
        XTE, AGG = psum[:, EB, 0:D], psum[:, AG, 0:D]

        ld_const, ld_edge, ld_seg, ld_w, ld_trow = (sem(s) for s in (
            "ld_const", "ld_edge", "ld_seg", "ld_w", "ld_trow"))
        prep = sem("prep")
        ends_out, ends_in, carry_out, carry_in = (sem(s) for s in (
            "ends_out", "ends_in", "carry_out", "carry_in"))
        ends_ready, carry_ready, memsets = sem("ends_ready"), sem("carry_ready"), sem("memsets")
        sums_ready, rows_ready, lin_out, ltile_in = (sem(s) for s in (
            "sums_ready", "rows_ready", "lin_out", "ltile_in"))
        ltr_ready, tables_ready, onehot_ready, w_ready, scan_ready = (sem(s) for s in (
            "ltr_ready", "tables_ready", "onehot_ready", "w_ready", "scan_ready"))
        fill_set, fill_out = sem("fill_set"), sem("fill_out")
        ltile_set = sem("ltile_set")
        x_in = sems("x_in", 2)
        y_out = sems("y_out", 2)
        xt_done, xt_copied, h_done, h_copied, z_done, z_added, sd_done, nb_done, y_done = (
            sem(s) for s in ("xt_done", "xt_copied", "h_done", "h_copied", "z_done", "z_added",
                             "sd_done", "nb_done", "y_done"))
        stats_done, aggr_done, rs_done = sem("stats_done"), sem("aggr_done"), sem("rs_done")

        class Edge:

            def __init__(self, ph):
                self.x_in = sems(f"{ph}_x_in", 4)
                self.a_in = sems(f"{ph}_a_in", 4) if ph == "b" else None
                self.tri = sem(f"{ph}_tri")
                self.smat = sem(f"{ph}_smat")
                self.wg = sem(f"{ph}_wg")
                self.xet = sem(f"{ph}_xet")
                self.xetc = sem(f"{ph}_xetc")
                self.mm = sem(f"{ph}_mm")
                self.hpre = sem(f"{ph}_hpre")
                self.prod = sem(f"{ph}_prod")
                self.red = sem(f"{ph}_red")
                self.carry = sem(f"{ph}_carry")
                self.agg = sem(f"{ph}_agg")
                self.aggc = sem(f"{ph}_aggc")
                self.out = sems(f"{ph}_out", 2)
                self.ixc = sem(f"{ph}_ixc")

        ea, eb = Edge("a"), Edge("b")
        slot_out = sems("slot_out", 4)
        slot_in = sems("slot_in", 4)
        c_x_in, c_a_in, c_y_out = sems("c_x_in", 4), sems("c_a_in", 4), sems("c_y_out", 4)
        (c_ixc, c_ixs, c_t1, c_t1c, c_m1, c_hp, c_h, c_t2, c_t2c, c_m2, c_xa, c_z, c_st, c_mv, c_sd, c_rs,
         c_nb, c_y) = (sem(f"c_{s}") for s in (
             "ixc", "ixs", "t1", "t1c", "m1", "hp", "h", "t2", "t2c", "m2", "xa", "z", "st", "mv", "sd",
             "rs", "nb", "y"))

        LD_CONST = 13 * 16

        def col(tensor, n):
            return tensor[:, bass.ds(n, 1)]

        def rows(table, n):
            return table[bass.ds(n * P, P), :]

        def group(table, g):
            return table[bass.ds(g * G, G), :].rearrange("(p j) d -> p j d", j=4)

        def tail(table):
            return table[NG * G:N, :].rearrange("(p j) d -> p j d", j=4)

        block = ctx.enter_context(nc.Block())

        @block.sync
        def _(sp):
            for dst_ap, src_ap in ((tri_sb[:, :], tri), (iota_sb[:, :], iota), (ppos_sb[:, :], ppos),
                                   (rel_sb[:, :], rel), (sel_sb[:, :], sel), (ident_sb[:, :], ident),
                                   (anti_sb[:, :], anti),
                                   (root1_sb[:, :, :], root1.rearrange("(k p) n -> p k n", p=P)),
                                   (root2_sb[:, :, :], root2.rearrange("(k p) n -> p k n", p=P)),
                                   (b1_col[:, :], b1), (first_carry[1:2, 0, :], b2[0:1, :]),
                                   (b2_row[:, :], b2[1:2, :].broadcast_to([3, D])),
                                   (first_carry[1:2, 1, :], b2[1:2, :])):
                sp.dma_start(dst_ap, src_ap).then_inc(ld_const, 16)
            for s in range(SEG):
                sp.dma_start(dseg[16 * s:16 * s + 16, :],
                             dstseg[s:s + 1, :].broadcast_to([16, SL + 2])).then_inc(ld_seg, 16)
                sp.dma_start(tseg[16 * s:16 * s + 16, :],
                             typseg[s:s + 1, :].broadcast_to([16, SL])).then_inc(ld_seg, 16)
            sp.dma_start(src_sb[:, :], src).then_inc(ld_edge, 16)
            sp.dma_start(dst_sb[:, :], dst).then_inc(ld_edge, 16)
            sp.dma_start(slotid_sb[:, :], slotid).then_inc(ld_edge, 16)
            sp.wait_ge(memsets, 1)
            for k in range(3):
                sp.dma_start(wf[32 * k:32 * k + 16, :], w1).then_inc(ld_w, 16)
            sp.wait_ge(fill_set, 1)
            sp.dma_start(node_slot.rearrange("(p k) o -> p (k o)", p=80), fill[:, :]).then_inc(fill_out, 16)
            sp.wait_ge(ends_ready, 1)
            sp.dma_start(seg_ends, ends[:, :]).then_inc(ends_out, 16)
            sp.wait_ge(ends_out, 16)
            sp.dma_start(ends_r[:, :, :], seg_ends.rearrange("(s r) q -> r s q", r=R)).then_inc(ends_in, 16)
            sp.wait_ge(carry_ready, 1)
            sp.dma_start(seg_carry.rearrange("(s r) q -> r s q", r=R), carry_r[:, :, :]).then_inc(carry_out, 16)
            sp.wait_ge(carry_out, 16)
            sp.dma_start(carry[:, :], seg_carry).then_inc(carry_in, 16)
            sp.wait_ge(w_ready, 1)
            for k in range(3):
                sp.dma_start(wf[32 * k:32 * k + 16, :], w2).then_inc(ld_w, 16)
            for k in range(TROWS):
                m = min(TROW, SLOTS - k * TROW)
                if k:
                    sp.wait_ge(onehot_ready, k)
                sp.dma_start(trow[:, 0:m], typ[0:1, k * TROW:k * TROW + m].broadcast_to([96, m])).then_inc(ld_trow, 16)
            for t in range(2):
                lin = (lin_len, lin_inv)[t]
                sp.dma_start(lin[E:LIN].rearrange("(o k) -> o k", o=1), pad_one[:, :]).then_inc(lin_out, 16)
            for t in range(2):
                sp.wait_ge(rows_ready, t + 1)
                lin = (lin_len, lin_inv)[t]
                sp.dma_start(lin[0:E].rearrange("(s k) -> s k", s=SEG), sums[t]).then_inc(lin_out, 16)
            sp.wait_ge(lin_out, 64)
            sp.wait_ge(ltile_set, 1)
            for t in range(2):
                lin = (lin_len, lin_inv)[t]
                for h, (c0, m) in enumerate(((0, P), (P, NCH - P))):
                    sp.dma_start(ltile[0:m, 2 * t + h, 2:P],
                                 lin[EC * c0:EC * (c0 + m)].rearrange("(c k) -> c k", k=EC)).then_inc(ltile_in, 16)
                    if t == 0:
                        sp.dma_start(ltile[0:m, h, 0:1],
                                     lin[EC * (c0 + 1):EC * (c0 + 1 + m)].rearrange("(c k) -> c k", k=EC)[:, 0:1],
                                     allow_slow_non_contiguous=True).then_inc(ltile_in, 16)

            def agg_store(e, table, n):
                sp.wait_ge(e.aggc, n.times(1, 1))
                sp.dma_start(rows(table, n.n), ao[:, n.at % 2, :]).then_inc(e.out[n.at % 2], 16)

            def y_store(g, m=P):
                sp.wait_ge(y_done, g.times(1, 1))
                sp.dma_start(group(y, g.n) if m == P else tail(y), zg[0:m, g.at % 2]).then_inc(y_out[g.at % 2], 16)

            def x_load(g, m=P):
                sp.wait_ge(z_added, g.times(2, -2))
                sp.dma_start(xg[0:m, g.at % 2], group(x, g.n) if m == P else tail(x)).then_inc(x_in[g.at % 2], 16)

            def step(e, table, n, g):
                if n.at > 0:
                    agg_store(e, table, n.plus(-1))
                if g is not None and not past(g.plus(2)):
                    x_load(g.plus(2), size(g.plus(2)))
                agg_store(e, table, n)
                if g is not None:
                    y_store(g, size(g))

            sp.wait_ge(tables_ready, 1)
            for u in range(2):
                sp.dma_start(xg[:, u], group(x, u)).then_inc(x_in[u], 16)
            phase_a(sp, lambda n, g: step(ea, agg1, n, g))
            agg_store(ea, agg1, Idx(NCH - 1))
            phase_b(sp, lambda n, g: step(eb, agg2, n, g))
            agg_store(eb, agg2, Idx(NCH - 1))
            sp.wait_ge(ea.out[0], 8 * NCH)
            sp.wait_ge(ea.out[1], 8 * NCH)
            sp.wait_ge(eb.out[0], 8 * NCH)
            sp.wait_ge(eb.out[1], 8 * NCH)

            def c_loads(n):
                r = n.at % 4
                if n.at >= 4:
                    sp.wait_ge(c_z, n.times(1, -3))
                sp.dma_start(a1l[:, r, :], rows(agg1, n.n)).then_inc(c_a_in[r], 16)
                sp.dma_start(a2l[:, r, :], rows(agg2, n.n)).then_inc(c_a_in[r], 16)

            for k in range(C_PRO):
                c_loads(Idx(k))
            with sp.Fori(0, C_IT) as i:
                for u in range(4):
                    c_loads(Idx(C_PRO + u, i))
            sp.wait_ge(y_out[0], 16 * ((NG + 2) // 2))
            sp.wait_ge(y_out[1], 16 * ((NG + 1) // 2))
            for r in range(4):
                sp.wait_ge(c_y_out[r], 4 * NCH)

        @block.gpsimd
        def _(pool):
            nc.gpsimd.memset(fill[:, :], 1).then_inc(fill_set, 1)
            pool.wait_ge(ld_edge, 48)
            pool.wait_ge(tables_ready, 1)
            pool.wait_ge(fill_out, 16)

            def column(n, kind, table, done):
                nc.gpsimd.tensor_copy(ix[:, kind, n.at % 4:n.at % 4 + 1], col(table, n.n)).then_inc(done, 1)

            last_node = nc.gpsimd.to_reg(N - 1)

            def gather(out_ap, table, index_ap, done):
                nc.gpsimd.indirect_dma_start(
                    out_ap, None, table, bass.IndirectOffsetOnAxis(ap=index_ap, axis=0),
                    bounds_check=last_node, oob_is_err=False).then_inc(done, 16)

            def scatter(table, index_ap, in_ap, done):
                nc.gpsimd.indirect_dma_start(
                    table, bass.IndirectOffsetOnAxis(ap=index_ap, axis=0), in_ap, None,
                    bounds_check=last_node, oob_is_err=False).then_inc(done, 16)

            def fours(first, last, chunk):
                for k in range(first, first + 4):
                    chunk(Idx(k))
                its = (last - first - 8) // 4
                with pool.Fori(0, its) as i:
                    for u in range(4):
                        chunk(Idx(first + 4 + u, i))
                for k in range(first + 4 + 4 * its, last):
                    chunk(Idx(k))

            def a_columns(n):
                column(n, 0, src_sb, ea.ixc)
                column(n, 1, first_dst, ea.ixc)
                column(n, 2, slotid_sb, ea.ixc)

            def a_chunk(n):
                r, ahead = n.at % 4, n.plus(1)
                if n.at >= 4:
                    pool.wait_ge(ea.prod, n.times(1, -3))
                if ahead.at >= 4:
                    pool.wait_ge(ea.x_in[ahead.at % 4], ahead.used(4))
                    pool.wait_ge(slot_out[ahead.at % 4], ahead.used(4))
                pool.wait_ge(ea.ixc, n.times(3, 3))
                if not past_chunks(ahead):
                    a_columns(ahead)
                gather(xe[:, r, :], x, ix[:, 0, r:r + 1], ea.x_in[r])
                scatter(node_slot, ix[:, 1, r:r + 1], ix[:, 2, r:r + 1], slot_out[r])

            a_columns(Idx(0))
            fours(0, NCH, a_chunk)

            for r in range(4):
                pool.wait_ge(slot_out[r], 4 * NCH)
                pool.wait_ge(ea.x_in[r], 4 * NCH)
            pool.wait_ge(ea.prod, NCH)
            pool.wait_ge(ea.out[0], 8 * NCH)
            pool.wait_ge(ea.out[1], 8 * NCH)

            def b_chunk(n):
                r, ahead, back = n.at % 4, n.plus(1), n.plus(-2)
                q = back.at % 4
                if n.at >= 4 and not past_chunks(n):
                    pool.wait_ge(eb.prod, n.times(1, -3))
                    pool.wait_ge(eb.a_in[r], n.used(4))
                if ahead.at >= 4 and not past_chunks(ahead):
                    pool.wait_ge(eb.x_in[ahead.at % 4], ahead.used(4))
                    pool.wait_ge(slot_in[ahead.at % 4], ahead.used(4))
                if not past_chunks(n):
                    pool.wait_ge(eb.ixc, n.times(1, 1))
                if back.at >= 0:
                    pool.wait_ge(slot_in[q], back.inn(4))
                if back.at >= 4:
                    pool.wait_ge(eb.hpre, back.times(1, -3))
                if not past_chunks(ahead):
                    column(ahead, 0, src_sb, eb.ixc)
                if not past_chunks(n):
                    gather(slot_ix[:, r:r + 1], node_slot, ix[:, 0, r:r + 1], slot_in[r])
                    gather(xe[:, r, :], x, ix[:, 0, r:r + 1], eb.x_in[r])
                if back.at >= 0:
                    gather(ae[:, q, :], agg1, slot_ix[:, q:q + 1], eb.a_in[q])

            column(Idx(0), 0, src_sb, eb.ixc)
            fours(0, NCH + 2, b_chunk)

            pool.wait_ge(eb.prod, NCH)
            for r in range(4):
                pool.wait_ge(eb.x_in[r], 4 * NCH)
            pool.wait_ge(y_out[0], 16 * ((NG + 2) // 2))
            pool.wait_ge(y_out[1], 16 * ((NG + 1) // 2))

            def c_chunk(n):
                r, ahead, back = n.at % 4, n.plus(1), n.plus(-C_LEAD)
                q, back1 = back.at % 4, back.plus(1)
                if n.at >= 4 and not past_chunks(n):
                    pool.wait_ge(c_xa, n.times(1, -3))
                    pool.wait_ge(c_t1, n.times(1, -3))
                if ahead.at >= 4 and not past_chunks(ahead):
                    pool.wait_ge(c_x_in[ahead.at % 4], ahead.used(4))
                if back1.at >= 4 and not past_chunks(back1):
                    pool.wait_ge(c_y_out[back1.at % 4], back1.used(4))
                if not past_chunks(n):
                    pool.wait_ge(c_ixc, n.times(1, 1))
                if back.at >= 0:
                    pool.wait_ge(c_ixs, back.times(1, 1))
                    pool.wait_ge(c_y, back.times(1, 1))
                if not past_chunks(ahead):
                    column(ahead, 0, first_dst, c_ixc)
                if back1.at >= 0 and not past_chunks(back1):
                    column(back1, 1, first_dst, c_ixs)
                if back.at >= 0:
                    scatter(y, ix[:, 1, q:q + 1], ze[:, q, :], c_y_out[q])
                if not past_chunks(n):
                    gather(xe[:, r, :], x, ix[:, 0, r:r + 1], c_x_in[r])

            column(Idx(0), 0, first_dst, c_ixc)
            for k in range(12):
                c_chunk(Idx(k))
            with pool.Fori(0, C_IT - 1) as i:
                for u in range(4):
                    c_chunk(Idx(12 + u, i))
            for k in range(NCH - 4, NCH + C_LEAD):
                c_chunk(Idx(k))

        @block.scalar
        def _(act):
            def relu(g, j, m=P):
                if g.at > 0 and j == 0:
                    act.wait_ge(z_done, g.times(2))
                act.wait_ge(h_done, g.times(2, 1 + j))
                nc.scalar.activation(ht[:, j, 0:4 * m], psum[:, HT[j], 0:4 * m], ACT.Relu,
                                     bias=b1_col[:, j:j + 1]).then_inc(h_copied, 1)

            def xt_copy(g, k, m=P):
                if g.at > 0 and k == 0:
                    act.wait_ge(h_done, g.times(2))
                act.wait_ge(xt_done, g.times(2, 1 + k))
                nc.scalar.copy(xt[:, k, 0:4 * m], psum[:, XT, 0:4 * m]).then_inc(xt_copied, 1)

            def deviation(g, m=P):
                act.wait_ge(aggr_done, g.times(4, 4))
                nc.scalar.activation(sd_d[0:m, :], mv_d[0:m, :, 1], ACT.Sqrt,
                                     bias=eps_col[0:m, :]).then_inc(sd_done, 1)

            def normalise(g, m=P):
                act.wait_ge(nb_done, g.times(1, 1))
                for t in range(4):
                    last = nc.scalar.activation(zg[0:m, g.at % 2, t, :], zg[0:m, g.at % 2, t, :],
                                                ACT.Identity, bias=nb_d[0:m, t:t + 1], scale=rs_d[0:m, t:t + 1])
                last.then_inc(y_done, 1)

            def scaled_triangle(e, n):
                if n.at >= 2:
                    act.wait_ge(e.smat, n.times(1, -1))
                nc.scalar.activation(tri_inv[:, n.at % 2, :], tri_sb[:, :], ACT.Copy,
                                     scale=col(inv_sb, n.n)).then_inc(e.tri, 1)

            def rows_t_copy(n):
                act.wait_ge(eb.xet, n.times(1, 1))
                if n.at >= 2:
                    act.wait_ge(eb.mm, n.times(1, -1))
                nc.scalar.copy(xet[:, n.at % 2, :], XTE).then_inc(eb.xetc, 1)

            def aggregate_copy(e, n):
                act.wait_ge(e.agg, n.times(1, 1))
                if n.at >= 2:
                    act.wait_ge(e.out[n.at % 2], n.used(2))
                    act.wait_ge(e.carry, n.n)
                nc.scalar.copy(ao[:, n.at % 2, :], AGG).then_inc(e.aggc, 1)

            def carry_rows(e, layer, n):
                act.wait_ge(e.red, n.times(1, 1))
                if n.at == 0:
                    source = first_carry[:, layer, :]
                else:
                    act.wait_ge(e.aggc, n.n)
                    source = ao[0:2, (n.at - 1) % 2, :]
                nc.scalar.copy(msg[0:2, n.at % 2, :], source).then_inc(e.carry, 1)

            def step(e, layer, n, g):
                n2 = n.plus(1)
                scaled_triangle(e, n2)
                if layer:
                    rows_t_copy(n2)
                carry_rows(e, layer, n)
                more = g is not None and not past(g.plus(1))
                if more:
                    relu(g.plus(1), 0, size(g.plus(1)))
                aggregate_copy(e, n)
                if g is not None:
                    deviation(g, size(g))
                if more:
                    relu(g.plus(1), 1, size(g.plus(1)))
                if not past_chunks(n.plus(2)):
                    scaled_triangle(e, n.plus(2))
                    if layer:
                        rows_t_copy(n.plus(2))
                if g is not None and not past(g.plus(2)):
                    xt_copy(g.plus(2), 0, size(g.plus(2)))
                    xt_copy(g.plus(2), 1, size(g.plus(2)))
                carry_rows(e, layer, n2)
                if g is not None:
                    normalise(g, size(g))
                aggregate_copy(e, n2)

            act.wait_ge(ld_const, LD_CONST)
            act.wait_ge(memsets, 1)
            act.wait_ge(tables_ready, 1)
            xt_copy(Idx(0), 0)
            xt_copy(Idx(0), 1)
            relu(Idx(0), 0)
            relu(Idx(0), 1)
            xt_copy(Idx(1), 0)
            xt_copy(Idx(1), 1)
            scaled_triangle(ea, Idx(0))
            phase_a(act, lambda n, g: step(ea, 0, n, g))
            act.wait_ge(ea.out[0], 8 * NCH)
            act.wait_ge(ea.out[1], 8 * NCH)
            scaled_triangle(eb, Idx(0))
            rows_t_copy(Idx(0))
            phase_b(act, lambda n, g: step(eb, 1, n, g))

            def c_t1_copy(n):
                act.wait_ge(c_t1, n.times(1, 1))
                if n.at >= 2:
                    act.wait_ge(c_m1, n.times(1, -1))
                nc.scalar.copy(xet[:, n.at % 2, :], psum[:, CT1[n.at % 2], 0:D]).then_inc(c_t1c, 1)

            def c_relu(n):
                act.wait_ge(c_hp, n.times(1, 1))
                if n.at >= 2:
                    act.wait_ge(c_t2, n.times(1, -1))
                nc.scalar.activation(he[:, n.at % 2, :], hpre[:, n.at % 2, :], ACT.Relu).then_inc(c_h, 1)

            def c_t2_copy(n):
                act.wait_ge(c_t2, n.times(1, 1))
                if n.at >= 2:
                    act.wait_ge(c_m2, n.times(1, -1))
                nc.scalar.copy(het[:, n.at % 2, :], psum[:, CT2[n.at % 2], 0:D]).then_inc(c_t2c, 1)

            def c_deviation(n):
                b = n.at % 2
                act.wait_ge(c_mv, n.times(1, 1))
                nc.scalar.activation(sd_e[:, b:b + 1], mv_e[:, b, 1:2], ACT.Sqrt,
                                     bias=eps_col[:, :]).then_inc(c_sd, 1)

            def c_normalise(n):
                b, r = n.at % 2, n.at % 4
                act.wait_ge(c_nb, n.times(1, 1))
                nc.scalar.activation(ze[:, r, :], ze[:, r, :], ACT.Identity, bias=nb_e[:, b:b + 1],
                                     scale=rs_e[:, b:b + 1]).then_inc(c_y, 1)

            c_slots(act, ((4, c_normalise), (2, c_t2_copy), (1, c_relu), (0, c_t1_copy), (3, c_deviation)))

        @block.vector
        def _(dve):
            steps = [0]

            def link(ins):
                steps[0] += 1
                ins.then_inc(prep, 1)
                dve.wait_ge(prep, steps[0])

            nc.vector.memset(eps_col[:, :], EPS)
            nc.vector.memset(ones3[:, :], 1.0)
            nc.vector.memset(pad_one[:, :], 1.0)
            nc.vector.memset(first_carry[0:1, :, :], 0.0)
            nc.vector.memset(wcat[:, :, :], 0.0)
            nc.vector.memset(wf[:, :], 0.0).then_inc(memsets, 1)
            nc.vector.memset(ltile[:, 0:2, 1:2], 1.0)
            nc.vector.memset(ltile[:, 2:4, 0:2], 1.0).then_inc(ltile_set, 1)

            def split_w(layer):
                dve.wait_ge(memsets, 1)
                dve.wait_ge(ld_w, 48 * (layer + 1))
                nc.vector.tensor_copy(wcat[0:16, layer, :], wf[0:16, :])
                for k in (1, 2):
                    p = slice(32 * k, 32 * k + 16)
                    link(nc.vector.tensor_copy(wcat[p, layer, :], wf[p, :]))
                    for _ in range(k - 1):
                        link(nc.vector.tensor_tensor(wf[p, :], wf[p, :], wcat[p, layer, :], ALU.subtract))
                        link(nc.vector.tensor_copy(wcat[p, layer, :], wf[p, :]))
                    link(nc.vector.tensor_tensor(wf[p, :], wf[p, :], wcat[p, layer, :], ALU.subtract))
                    last = nc.vector.tensor_copy(wcat[p, layer, :], wf[p, :])
                last.then_inc(w_ready, 1)
                dve.wait_ge(w_ready, layer + 1)

            dve.wait_ge(ld_seg, 256)
            dve.wait_ge(ld_const, LD_CONST)
            link(nc.vector.tensor_tensor(same[:, :], dseg[:, 0:SL + 1], dseg[:, 1:SL + 2], ALU.is_equal))
            link(nc.vector.tensor_scalar(oh[:, :], tseg[:, :], rel_sb[:, 0:1], None, ALU.is_equal))
            into, onto = same[:, 0:SL], same[:, 1:SL + 1]
            link(nc.vector.tensor_tensor_scan(fwd[:, :], into, oh[:, :], 0.0, ALU.mult, ALU.add))
            link(nc.vector.tensor_tensor_scan(bwd[:, ::-1], onto[:, ::-1], oh[:, ::-1], 0.0, ALU.mult, ALU.add))
            link(nc.vector.tensor_copy(ends[:, 0:1], fwd[:, SL - 1:SL]))
            link(nc.vector.tensor_copy(ends[:, 2:3], bwd[:, 0:1]))
            link(nc.vector.tensor_reduce(ends[:, 1:2], into, AX.X, ALU.min))
            nc.vector.tensor_reduce(ends[:, 3:4], onto, AX.X, ALU.min).then_inc(ends_ready, 1)
            split_w(0)
            dve.wait_ge(ends_in, 16)
            link(nc.vector.memset(carry_r[:, 0:1, 0:1], 0.0))
            link(nc.vector.memset(carry_r[:, SEG - 1:SEG, 1:2], 0.0))
            link(nc.vector.tensor_tensor_scan(carry_r[:, 1:SEG, 0], ends_r[:, 0:SEG - 1, 1],
                                              ends_r[:, 0:SEG - 1, 0], 0.0, ALU.mult, ALU.add))
            nc.vector.tensor_tensor_scan(carry_r[:, 0:SEG - 1, 1][:, ::-1], ends_r[:, 1:SEG, 3][:, ::-1],
                                         ends_r[:, 1:SEG, 2][:, ::-1], 0.0, ALU.mult, ALU.add).then_inc(carry_ready, 1)
            link(nc.vector.tensor_tensor_scan(cont[:, :], into, into, 1.0, ALU.mult, ALU.min))
            dve.wait_ge(carry_in, 16)
            link(nc.vector.scalar_tensor_tensor(fwd[:, :], cont[:, :], carry[:, 0:1], fwd[:, :], ALU.mult, ALU.add))
            link(nc.vector.tensor_tensor_scan(cont[:, ::-1], onto[:, ::-1], onto[:, ::-1], 1.0, ALU.mult, ALU.min))
            link(nc.vector.scalar_tensor_tensor(bwd[:, :], cont[:, :], carry[:, 1:2], bwd[:, :], ALU.mult, ALU.add))
            link(nc.vector.tensor_tensor(bwd[:, :], fwd[:, :], bwd[:, :], ALU.add))
            nc.vector.scalar_tensor_tensor(bwd[:, :], bwd[:, :], -1.0, oh[:, :], ALU.add, ALU.mult).then_inc(scan_ready, 1)
            split_w(1)
            dve.wait_ge(sums_ready, 1)
            for k in range(PIECES):
                m = min(512, SL - 512 * k)
                last = nc.vector.tensor_copy(sums[0][:, 512 * k:512 * k + m], psum[0:SEG, k, 0:m])
            last.then_inc(rows_ready, 1)
            dve.wait_ge(sums_ready, 2)
            for k in range(PIECES):
                m = min(512, SL - 512 * k)
                last = nc.vector.reciprocal(sums[1][:, 512 * k:512 * k + m], psum[0:SEG, k, 0:m])
            last.then_inc(rows_ready, 1)
            for k in range(TROWS):
                m = min(TROW, SLOTS - k * TROW)
                dve.wait_ge(ld_trow, 16 * (k + 1))
                nc.vector.tensor_scalar(onehot[:, k * TROW:k * TROW + m], trow[:, 0:m], rel_sb[0:96, 1:2], None,
                                        ALU.is_equal).then_inc(onehot_ready, 1)
            link(nc.vector.tensor_copy(b2_parts[:, 0, :], b2_row[:, :]))
            link(nc.vector.tensor_tensor(b2_res[:, :], b2_row[:, :], b2_parts[:, 0, :], ALU.subtract))
            link(nc.vector.tensor_copy(b2_parts[:, 1, :], b2_res[:, :]))
            link(nc.vector.tensor_tensor(b2_res[:, :], b2_res[:, :], b2_parts[:, 1, :], ALU.subtract))
            link(nc.vector.tensor_copy(b2_parts[:, 2, :], b2_res[:, :]))
            link(nc.vector.tensor_scalar(b2_sel[:, :], b2_parts[:, 0, :], ident_sb[0:3, 0:1], None, ALU.mult))
            for k in (1, 2):
                link(nc.vector.scalar_tensor_tensor(b2_sel[:, :], b2_parts[:, k, :], ident_sb[0:3, k:k + 1],
                                                    b2_sel[:, :], ALU.mult, ALU.add))
            link(nc.vector.tensor_copy(b2_bf[:, 0, :], b2_sel[:, :]))
            link(nc.vector.tensor_copy(b2_bf[:, 1, :], b2_sel[:, :]))
            dve.wait_ge(ltr_ready, 1)
            dve.wait_ge(ld_edge, 48)
            link(nc.vector.tensor_copy(len_sb[:, :], psum[:, 0, 0:NCH]))
            link(nc.vector.tensor_copy(inv_sb[:, :], psum[:, 1, 0:NCH]))
            link(nc.vector.tensor_scalar(start_sb[:, :], len_sb[:, :], -1.0, ppos_sb[:, 0:1], ALU.mult, ALU.add))
            link(nc.vector.tensor_scalar(later[:, :], len_sb[:, :], 1.0, float(BIG), ALU.is_gt, ALU.mult))
            nc.vector.tensor_tensor(first_dst[:, :], dst_sb[:, :], later[:, :], ALU.add).then_inc(tables_ready, 1)

            def add_x(g, q, m=P):
                b = g.at % 2
                dve.wait_ge(z_done, g.times(2, 1 + q))
                if g.at >= 2 and q == 0:
                    dve.wait_ge(y_out[b], g.used(2))
                nc.vector.tensor_tensor(zg[0:m, b, 2 * q:2 * q + 2, :].rearrange("p t d -> p (t d)"),
                                        psum[0:m, ZB, :],
                                        xg[0:m, b, 2 * q:2 * q + 2, :].rearrange("p t d -> p (t d)"),
                                        ALU.add).then_inc(z_added, 1)
                dve.wait_ge(z_added, g.times(2, 1 + q))
                if g.at >= 1 and q == 0:
                    dve.wait_ge(aggr_done, g.times(4))
                for t in (2 * q, 2 * q + 1):
                    nc.vector.bn_stats(st_d[0:m, t, :], zg[0:m, b, t, :]).then_inc(stats_done, 1)

            def before_moments(g):
                dve.wait_ge(stats_done, g.times(4, 4))
                if g.at >= 1:
                    dve.wait_ge(nb_done, g.n)

            def moments(g, m=P):
                for t in range(4):
                    nc.vector.bn_aggr(mv_d[0:m, t, :], st_d[0:m, t, :]).then_inc(aggr_done, 1)

            def scales(g, m=P):
                dve.wait_ge(sd_done, g.times(1, 1))
                if g.at >= 1:
                    dve.wait_ge(y_done, g.n)
                nc.vector.reciprocal(rs_d[0:m, :], sd_d[0:m, :]).then_inc(rs_done, 1)
                dve.wait_ge(rs_done, g.times(1, 1))
                nc.vector.scalar_tensor_tensor(nb_d[0:m, :], mv_d[0:m, :, 0], -1.0, rs_d[0:m, :], ALU.mult,
                                               ALU.mult).then_inc(nb_done, 1)

            def suffix_matrix(e, n):
                b = n.at % 2
                dve.wait_ge(e.tri, n.times(1, 1))
                if n.at >= 2:
                    dve.wait_ge(e.agg, n.times(1, -1))
                nc.vector.scalar_tensor_tensor(smat[:, b, :], iota_sb[:, :], col(start_sb, n.n), tri_inv[:, b, :],
                                               ALU.is_ge, ALU.mult).then_inc(e.smat, 1)

            def messages(e, layer, n):
                b, r = n.at % 2, n.at % 4
                if layer:
                    dve.wait_ge(eb.a_in[r], n.inn(4))
                    dve.wait_ge(eb.mm, n.times(1, 1))
                    if n.at >= 2:
                        dve.wait_ge(eb.prod, n.times(1, -1))
                    nc.vector.tensor_tensor(hpre[:, b, :], XTE, ae[:, r, :], ALU.add).then_inc(eb.hpre, 1)
                    dve.wait_ge(eb.hpre, n.times(1, 1))
                    row, least = hpre[:, b, :], 0.0
                else:
                    dve.wait_ge(ea.x_in[r], n.inn(4))
                    row, least = xe[:, r, :], None
                dve.wait_ge(e.wg, n.times(1, 1))
                if n.at >= 2:
                    dve.wait_ge(e.red, n.times(1, -1))
                four = row.unsqueeze(1).broadcast_to([P, 4, D])
                out_ap = prod[:, b, :].rearrange("p (o k) -> p o k", o=4)
                w_ap = psum[:, WG:WG + 2, :].rearrange("p a (h k) -> p (a h) k", h=2)
                nc.vector.scalar_tensor_tensor(out_ap, four, 1.0 if least is None else least, w_ap,
                                               ALU.mult if least is None else ALU.max,
                                               ALU.mult).then_inc(e.prod, 1)
                dve.wait_ge(e.prod, n.times(1, 1))
                nc.vector.tensor_reduce(msg[:, b, :].rearrange("p (b o) -> p o b", o=4),
                                        prod[:, b, :].rearrange("p (o b i) -> p o b i", o=4, i=4),
                                        AX.X, ALU.add).then_inc(e.red, 1)

            def step(e, layer, n, g):
                suffix_matrix(e, n)
                messages(e, layer, n)
                if g is not None:
                    add_x(g, 1, size(g))
                    before_moments(g)
                suffix_matrix(e, n.plus(1))
                if g is not None:
                    moments(g, size(g))
                messages(e, layer, n.plus(1))
                if g is not None:
                    scales(g, size(g))
                    if not past(g.plus(1)):
                        add_x(g.plus(1), 0, size(g.plus(1)))

            add_x(Idx(0), 0)
            phase_a(dve, lambda n, g: step(ea, 0, n, g))
            dve.wait_ge(ea.agg, NCH)
            dve.wait_ge(ea.red, NCH)
            phase_b(dve, lambda n, g: step(eb, 1, n, g))
            dve.wait_ge(eb.prod, NCH)

            def c_add_agg1(n):
                b, r = n.at % 2, n.at % 4
                dve.wait_ge(c_m1, n.times(1, 1))
                dve.wait_ge(c_a_in[r], two(n))
                if n.at >= 2:
                    dve.wait_ge(c_h, n.times(1, -1))
                nc.vector.tensor_tensor(hpre[:, b, :], psum[:, CM1[b], 0:D], a1l[:, r, :], ALU.add).then_inc(c_hp, 1)

            def c_add_agg2(n):
                b = r = n.at % 4
                dve.wait_ge(c_a_in[r], two(n))
                dve.wait_ge(c_x_in[r], n.inn(4))
                if n.at >= 4:
                    dve.wait_ge(c_z, n.times(1, -3))
                nc.vector.tensor_tensor(xa[:, b, :], xe[:, r, :], a2l[:, r, :], ALU.add).then_inc(c_xa, 1)

            def c_statistics(n):
                b, r = n.at % 2, n.at % 4
                dve.wait_ge(c_m2, n.times(1, 1))
                dve.wait_ge(c_xa, n.times(1, 1))
                if n.at >= 4:
                    dve.wait_ge(c_y_out[r], n.used(4))
                nc.vector.tensor_tensor(ze[:, r, :], psum[:, CM2[b], 0:D], xa[:, r, :], ALU.add).then_inc(c_z, 1)
                dve.wait_ge(c_z, n.times(1, 1))
                if n.at >= 2:
                    dve.wait_ge(c_mv, n.times(1, -1))
                nc.vector.bn_stats(st_e[:, b, :], ze[:, r, :]).then_inc(c_st, 1)
                dve.wait_ge(c_st, n.times(1, 1))
                if n.at >= 2:
                    dve.wait_ge(c_nb, n.times(1, -1))

            def c_moments(n):
                b = n.at % 2
                nc.vector.bn_aggr(mv_e[:, b, :], st_e[:, b, :]).then_inc(c_mv, 1)

            def c_scale(n):
                b = n.at % 2
                dve.wait_ge(c_sd, n.times(1, 1))
                if n.at >= 2:
                    dve.wait_ge(c_y, n.times(1, -1))
                nc.vector.reciprocal(rs_e[:, b:b + 1], sd_e[:, b:b + 1]).then_inc(c_rs, 1)
                dve.wait_ge(c_rs, n.times(1, 1))
                nc.vector.scalar_tensor_tensor(nb_e[:, b:b + 1], mv_e[:, b, 0:1], -1.0, rs_e[:, b:b + 1], ALU.mult,
                                               ALU.mult).then_inc(c_nb, 1)

            c_slots(dve, ((4, c_scale), (3, c_statistics), (1, c_add_agg1), (3, c_moments), (0, c_add_agg2)))

        @block.tensor
        def _(pe):
            def transpose_x(g, k, m=P):
                b = g.at % 2
                pe.wait_ge(x_in[b], g.inn(2))
                if g.at > 0 or k > 0:
                    pe.wait_ge(xt_copied, g.times(2, k))
                for t in range(4):
                    last = nc.tensor.transpose(psum[:, XT, t * m:(t + 1) * m],
                                               xg[0:m, b, t, k * P:(k + 1) * P], ident_sb[0:m, 0:m])
                last.then_inc(xt_done, 1)

            def layer1(g, j, m=P):
                pe.wait_ge(xt_copied, g.times(2, 2))
                if g.at > 0:
                    pe.wait_ge(h_copied, g.times(2, -1 + j))
                for k in range(2):
                    last = nc.tensor.matmul(psum[:, HT[j], 0:4 * m], root1_sb[:, k, j * P:(j + 1) * P],
                                            xt[:, k, 0:4 * m], start=(k == 0), stop=(k == 1))
                last.then_inc(h_done, 1)

            def layer2(g, q, m=P):
                pe.wait_ge(h_copied, g.times(2, 2))
                if g.at > 0 or q > 0:
                    pe.wait_ge(z_added, g.times(2, q))
                nc.tensor.matmul(psum[0:m, ZB, :], ones3[:, 0:m], b2_bf[:, :, :].rearrange("p a d -> p (a d)"),
                                 start=True, stop=False)
                for a in range(2):
                    t = 2 * q + a
                    for j in range(2):
                        last = nc.tensor.matmul(psum[0:m, ZB, a * D:(a + 1) * D], ht[:, j, t * m:(t + 1) * m],
                                                root2_sb[:, j, :], start=False, stop=(a == 1 and j == 1))
                last.then_inc(z_done, 1)

            def slot_weights(e, layer, n):
                if n.at > 0:
                    pe.wait_ge(e.prod, n.n)
                hot = onehot[:, bass.ds(n.n * P, P)]
                for h in range(2):
                    last = nc.tensor.matmul(psum[:, WG + h, :], hot, wcat[:, layer, 512 * h:512 * (h + 1)],
                                            start=True, stop=True)
                last.then_inc(e.wg, 1)

            def transpose_rows(n):
                r = n.at % 4
                pe.wait_ge(eb.x_in[r], n.inn(4))
                if n.at > 0:
                    pe.wait_ge(eb.hpre, n.n)
                for k in range(2):
                    last = nc.tensor.transpose(psum[:, EB, k * P:(k + 1) * P], xe[:, r, k * P:(k + 1) * P],
                                               ident_sb[:, :])
                last.then_inc(eb.xet, 1)

            def source_layer1(n):
                pe.wait_ge(eb.xetc, n.times(1, 1))
                for k in range(2):
                    last = nc.tensor.matmul(XTE, xet[:, n.at % 2, k * P:(k + 1) * P], root1_sb[:, k, :],
                                            start=(k == 0), stop=(k == 1))
                last.then_inc(eb.mm, 1)

            def aggregate(e, n):
                b = n.at % 2
                pe.wait_ge(e.carry, n.times(1, 1))
                pe.wait_ge(e.smat, n.times(1, 1))
                if n.at > 0:
                    pe.wait_ge(e.aggc, n.n)
                nc.tensor.matmul(AGG, smat[:, b, :], msg[:, b, :], start=True, stop=True).then_inc(e.agg, 1)

            def step(e, layer, n, g):
                n2, n3 = n.plus(1), n.plus(2)
                if g is not None:
                    layer2(g, 1, size(g))
                if layer:
                    transpose_rows(n2)
                slot_weights(e, layer, n2)
                more = g is not None and not past(g.plus(1))
                if more:
                    layer1(g.plus(1), 0, size(g.plus(1)))
                if layer:
                    source_layer1(n2)
                aggregate(e, n)
                if more:
                    layer1(g.plus(1), 1, size(g.plus(1)))
                if not past_chunks(n3):
                    if layer:
                        transpose_rows(n3)
                    slot_weights(e, layer, n3)
                more2 = g is not None and not past(g.plus(2))
                if more2:
                    transpose_x(g.plus(2), 0, size(g.plus(2)))
                if more:
                    layer2(g.plus(1), 0, size(g.plus(1)))
                if more2:
                    transpose_x(g.plus(2), 1, size(g.plus(2)))
                if layer and not past_chunks(n3):
                    source_layer1(n3)
                aggregate(e, n2)

            pe.wait_ge(ld_const, LD_CONST)
            pe.wait_ge(scan_ready, 1)
            for t, what in enumerate((fwd, bwd)):
                if t:
                    pe.wait_ge(rows_ready, 1)
                for k in range(PIECES):
                    m = min(512, SL - 512 * k)
                    last = nc.tensor.matmul(psum[0:SEG, k, 0:m], sel_sb[:, :], what[:, 512 * k:512 * k + m],
                                            start=True, stop=True)
                last.then_inc(sums_ready, 1)
            pe.wait_ge(ltile_in, 96)
            pe.wait_ge(rows_ready, 2)
            for t in range(2):
                for h, (m, n0) in enumerate(((P, NCH - P), (NCH - P, 0))):
                    last = nc.tensor.transpose(psum[:, t, n0:n0 + m], ltile[0:m, 2 * t + h, :],
                                               anti_sb[0:m, P - m:P])
            last.then_inc(ltr_ready, 1)
            pe.wait_ge(tables_ready, 1)
            pe.wait_ge(onehot_ready, TROWS)
            transpose_x(Idx(0), 0)
            transpose_x(Idx(0), 1)
            layer1(Idx(0), 0)
            layer1(Idx(0), 1)
            transpose_x(Idx(1), 0)
            layer2(Idx(0), 0)
            transpose_x(Idx(1), 1)
            slot_weights(ea, 0, Idx(0))
            phase_a(pe, lambda n, g: step(ea, 0, n, g))
            pe.wait_ge(ea.prod, NCH)
            pe.wait_ge(ea.aggc, NCH)
            transpose_rows(Idx(0))
            slot_weights(eb, 1, Idx(0))
            source_layer1(Idx(0))
            phase_b(pe, lambda n, g: step(eb, 1, n, g))
            pe.wait_ge(z_added, 2 * (NG + 1))
            pe.wait_ge(eb.aggc, NCH)
            pe.wait_ge(eb.prod, NCH)

            def c_transpose_x(n):
                b, r = n.at % 2, n.at % 4
                pe.wait_ge(c_x_in[r], n.inn(4))
                if n.at >= 2:
                    pe.wait_ge(c_t1c, n.times(1, -1))
                for k in range(2):
                    last = nc.tensor.transpose(psum[:, CT1[b], k * P:(k + 1) * P], xe[:, r, k * P:(k + 1) * P],
                                               ident_sb[:, :])
                last.then_inc(c_t1, 1)

            def c_layer1(n):
                b = n.at % 2
                pe.wait_ge(c_t1c, n.times(1, 1))
                if n.at >= 2:
                    pe.wait_ge(c_hp, n.times(1, -1))
                for k in range(2):
                    last = nc.tensor.matmul(psum[:, CM1[b], 0:D], xet[:, b, k * P:(k + 1) * P], root1_sb[:, k, :],
                                            start=(k == 0), stop=(k == 1))
                last.then_inc(c_m1, 1)

            def c_transpose_h(n):
                b = n.at % 2
                pe.wait_ge(c_h, n.times(1, 1))
                if n.at >= 2:
                    pe.wait_ge(c_t2c, n.times(1, -1))
                for k in range(2):
                    last = nc.tensor.transpose(psum[:, CT2[b], k * P:(k + 1) * P], he[:, b, k * P:(k + 1) * P],
                                               ident_sb[:, :])
                last.then_inc(c_t2, 1)

            def c_layer2(n):
                b = n.at % 2
                pe.wait_ge(c_t2c, n.times(1, 1))
                if n.at >= 2:
                    pe.wait_ge(c_z, n.times(1, -1))
                for k in range(2):
                    last = nc.tensor.matmul(psum[:, CM2[b], 0:D], het[:, b, k * P:(k + 1) * P], root2_sb[:, k, :],
                                            start=(k == 0), stop=(k == 1))
                last.then_inc(c_m2, 1)

            c_slots(pe, ((3, c_layer2), (2, c_transpose_h), (1, c_layer1), (0, c_transpose_x)))


def size(g):
    return RP if g.i is None and g.at == NG else P


def past(g):
    return g.i is None and g.at > NG


def past_chunks(n):
    return n.i is None and n.at >= NCH


def phase_a(eng, step):
    for k in range(PRO // 2):
        step(Idx(2 * k), Idx(k))
    with eng.Fori(0, A_IT - 1) as i:
        for v in range(2):
            step(Idx(PRO + 2 * v, i), Idx(A_G + v, i, 2))
    for v in range(2):
        step(Idx(NCH - 4 + 2 * v), Idx(A_G + 2 * A_IT - 2 + v))


def phase_b(eng, step):
    for k in range(PRO // 2):
        step(Idx(2 * k), None)
    with eng.Fori(0, B_IT) as i:
        for v in range(2):
            step(Idx(PRO + 2 * v, i), Idx(A_G + 2 * A_IT + v, i, 2))
    for k in range(4):
        step(Idx(NCH - 8 + 2 * k), Idx(NG - 3 + k))


def c_slots(eng, stages):
    lag = max(k for k, _ in stages)
    for n in range(C_PRO):
        for k, stage in stages:
            if n >= k:
                stage(Idx(n - k))
    with eng.Fori(0, C_IT) as i:
        for u in range(4):
            for k, stage in stages:
                stage(Idx(C_PRO + u - k, i))
    for n in range(NCH, NCH + lag):
        for k, stage in stages:
            if n - k < NCH:
                stage(Idx(n - k))


def two(n):
    return n.at // 4 * 32 + 32 if n.i is None else n.i * 32 + (n.at // 4 * 32 + 32)


def kernel(x, src, dst, edge_type_16, L0_gnn_W1, L0_gnn_root1, L0_gnn_bias1, L0_gnn_W2, L0_gnn_root2, L0_gnn_bias2):
    import numpy as np
    import concourse.bacc as bacc
    from concourse.bass_utils import run_bass_kernel_spmd

    def slots(a, fill):
        a = np.asarray(a)
        out = np.full((NCH, P), fill, a.dtype)
        padded = np.full(NCH * EC, fill, a.dtype)
        padded[:E] = a
        out[:, 2:] = padded.reshape(NCH, EC)[::-1]
        return out

    src, dst, typ = (np.asarray(a) for a in (src, dst, edge_type_16))
    around = np.full(E + 2, -1, dst.dtype)
    around[1:-1] = dst
    ar = np.arange(P)
    f = np.float32
    tri = (ar[:, None] >= ar[None, :]).astype(f)
    tri[:, 0] = 1
    tri[0, :] = 1
    tri[:, 1] = 0
    tri[0, 1] = 0
    tri[1, :] = 1
    tri[1, 0] = 0
    iota = np.tile(ar.astype(f), (P, 1))
    iota[:, 0] = 2
    ppos = (ar + 1).astype(f).reshape(P, 1)
    ppos[0] = P + 1
    arrays = dict(
        x=np.asarray(x),
        src=np.ascontiguousarray(slots(src, 0).T), dst=np.ascontiguousarray(slots(dst, BIG).T),
        typ=slots(typ, 0).reshape(1, SLOTS),
        dstseg=np.stack([around[s * SL:s * SL + SL + 2] for s in range(SEG)]),
        typseg=typ.reshape(SEG, SL),
        w1=np.ascontiguousarray(np.asarray(L0_gnn_W1).transpose(0, 3, 1, 2)).reshape(R, 4 * D),
        w2=np.ascontiguousarray(np.asarray(L0_gnn_W2).transpose(0, 3, 1, 2)).reshape(R, 4 * D),
        root1=np.asarray(L0_gnn_root1), root2=np.asarray(L0_gnn_root2),
        b1=np.ascontiguousarray(np.asarray(L0_gnn_bias1).reshape(2, P).T),
        b2=np.stack([np.asarray(L0_gnn_bias1), np.asarray(L0_gnn_bias2)]),
        tri=tri, iota=iota, ppos=ppos,
        rel=np.stack([ar % 16, ar % 32], 1).astype(f),
        sel=(ar[:, None] // 16 == np.arange(SEG)[None, :]).astype(f),
        ident=np.eye(P, dtype=f), anti=np.ascontiguousarray(np.eye(P, dtype=f)[::-1]),
        slotid=np.ascontiguousarray(np.arange(SLOTS, dtype=np.int32).reshape(NCH, P).T),
    )
    nc = bacc.Bacc("TRN2", target_bir_lowering=False, num_devices=1)
    args = {k: nc.dram_tensor(f"in_{k}", a.shape, mybir.dt.from_np(a.dtype), kind="ExternalInput").ap()
            for k, a in arrays.items()}
    y = nc.dram_tensor("out_y", (N, D), F32, kind="ExternalOutput").ap()
    program(nc, **args, y=y)
    r = run_bass_kernel_spmd(nc, [{f"in_{k}": a for k, a in arrays.items()}], core_ids=[0])
    return r.results[0]["out_y"]
```

```python
from contextlib import ExitStack

import concourse.bass as bass
from concourse import mybir
from concourse.alu_op_type import AluOpType as ALU

N, D, E, R = 100000, 256, 25000, 16
P = 128
EC = P - 2
NCH = -(-E // (4 * EC)) * 4
SLOTS = NCH * P
BIG = 1 << 20
SEG = 8
SL = E // SEG
LIN = EC * (NCH + 1)
G = 512
NG = N // G
REM = N - NG * G
RP = REM // 4
PRO = 8
A_IT = (NCH - 2 * PRO) // 8
A_G = NCH // 2
B_IT = (NG + 1 - A_G - 4) // 4
C_PRO = 12
C_IT = (NCH - C_PRO) // 4
C_LEAD = 6
EP = -(-E // P)
NLIN = NCH * EC + 2
EPS = 1e-5
PIECES = -(-SL // 512)
TROW = 640
TROWS = (SLOTS - 2 * SL) // TROW + 1
TLAST = SLOTS - TROWS * TROW
assert C_PRO + 4 * C_IT == NCH
assert 2 * PRO + 8 * A_IT == NCH and B_IT == A_IT and A_G + 4 * B_IT + 4 == NG + 1
A_LEAD, B_LEAD = 3, 4
F32, F32R, BF16, I32 = mybir.dt.float32, mybir.dt.float32r, mybir.dt.bfloat16, mybir.dt.int32
ACT = mybir.ActivationFunctionType
AX = mybir.AxisListType


class Idx:

    def __init__(self, at, i=None, by=4):
        self.at, self.i, self.by = at, i, by
        self.n = at if i is None else i * by + at

    def plus(self, k):
        return Idx(self.at + k, self.i, self.by)

    def times(self, k, more=0):
        return self.at * k + more if self.i is None else self.i * (self.by * k) + (self.at * k + more)

    def used(self, k):
        return self.at // k * 16 if self.i is None else self.i * (self.by // k * 16) + self.at // k * 16

    def inn(self, k):
        return self.at // k * 16 + 16 if self.i is None else self.i * (self.by // k * 16) + (self.at // k * 16 + 16)


def program(nc, x, src, dst, typ, dstseg, typseg, edges, eidx, along, blank, w1, w2, root1, root2, b2, tri, iota, ppos,
            rel, sel, ident, anti, slotid, y):
    ctx = ExitStack()
    with ctx:
        def sb(name, shape, dt=F32):
            return ctx.enter_context(nc.sbuf_tensor(name, shape, dt))

        def sem(name):
            return ctx.enter_context(nc.semaphore(name))

        def sems(name, n):
            return [sem(f"{name}{k}") for k in range(n)]

        seg_ends = nc.dram_tensor("seg_ends", (P, 4), F32).ap()
        seg_carry = nc.dram_tensor("seg_carry", (P, 2), F32).ap()
        lin_count = nc.dram_tensor("lin_count", (LIN,), F32).ap()
        lin_len = nc.dram_tensor("lin_len", (LIN,), F32).ap()
        node_slot = nc.dram_tensor("node_slot", (N, 1), I32).ap()
        dst_lin, typ_lin, src_lin = (nc.dram_tensor(s, (NLIN, 1), I32).ap()
                                     for s in ("dst_lin", "typ_lin", "src_lin"))
        typ_slots = nc.dram_tensor("typ_slots", (NCH, P), I32).ap()
        agg1 = nc.dram_tensor("agg1", (SLOTS, D), F32).ap()
        agg2 = nc.dram_tensor("agg2", (SLOTS, D), F32).ap()

        root1_sb = sb("root1_sb", [P, 2, D])
        root2_sb = sb("root2_sb", [P, 2, D])
        root1_hi, root1_lo, root2_hi, root2_lo = (
            sb(s, [P, 2, D], F32R) for s in ("root1_hi", "root1_lo", "root2_hi", "root2_lo"))
        bias_row = sb("bias_row", [3, 2 * D])
        bias_res = sb("bias_res", [3, 2 * D])
        bias_parts = sb("bias_parts", [3, 3, 2 * D], BF16)
        bias_sel = sb("bias_sel", [3, 2 * D])
        b1_bf = sb("b1_bf", [3, D], BF16)
        b2_bf = sb("b2_bf", [3, 2, D], BF16)
        ones3 = sb("ones3", [3, G], BF16)
        first_carry = sb("first_carry", [2, 2, D])
        tri_sb = sb("tri_sb", [P, P])
        iota_sb = sb("iota_sb", [P, P])
        ppos_sb = sb("ppos_sb", [P, 1])
        rel_sb = sb("rel_sb", [P, 2])
        sel_sb = sb("sel_sb", [P, SEG])
        ident_sb = sb("ident_sb", [P, P])
        anti_sb = sb("anti_sb", [P, P])
        eps_col = sb("eps_col", [P, 1])
        wcat = sb("wcat", [96, 2, 4 * D], BF16)
        wf = sb("wf", [96, 4 * D])
        xt_hi, xt_lo, ht_hi, ht_lo = (
            sb(s, [P, 2, G], F32R) for s in ("xt_hi", "xt_lo", "ht_hi", "ht_lo"))
        src_sb = sb("src_sb", [P, NCH], I32)
        dst_sb = sb("dst_sb", [P, NCH], I32)
        slotid_sb = sb("slotid_sb", [P, NCH], I32)
        onehot = sb("onehot", [96, SLOTS], BF16)
        inv_sb = sb("inv_sb", [P, NCH])
        len_sb = sb("len_sb", [P, NCH])
        start_sb = sb("start_sb", [P, NCH])
        later = sb("later", [P, NCH])
        first_dst = sb("first_dst", [P, NCH], I32)
        trow = sb("trow", [96, 2, TROW], I32)
        ends = sb("ends", [P, 4])
        ends_r = sb("ends_r", [R, SEG, 4])
        carry_r = sb("carry_r", [R, SEG, 2])
        carry = sb("carry", [P, 2])
        ltile = sb("ltile", [P, 4, P])
        descents, ones_col, unsorted = sb("descents", [P, 1]), sb("ones_col", [P, 1]), sb("unsorted", [1, 1], I32)
        rank_ix, rec_ix = sb("rank_ix", [P, 1], I32), sb("rec_ix", [P, 3], I32)
        fill = sb("fill", [80, N // 80], I32)
        pad_one = sb("pad_one", [1, LIN - E])
        st_d = sb("st_d", [P, 4, 6])
        mv_d = sb("mv_d", [P, 4, 2])
        sd_d, rs_d, nb_d = (sb(s, [P, 4]) for s in ("sd_d", "rs_d", "nb_d"))
        ix = sb("ix", [P, 3, 4], I32)
        slot_ix = sb("slot_ix", [P, 4], I32)
        st_e = sb("st_e", [P, 2, 6])
        mv_e = sb("mv_e", [P, 2, 2])
        sd_e, rs_e, nb_e = (sb(s, [P, 2]) for s in ("sd_e", "rs_e", "nb_e"))

        work = sb("work", [P, 7 * (SL + 2)])

        def carver():
            at = [0]

            def carve(*shape):
                size = 1
                for k in shape:
                    size *= k
                flat = work[:, at[0]:at[0] + size]
                at[0] += size
                assert at[0] <= 7 * (SL + 2)
                if len(shape) == 1:
                    return flat
                if len(shape) == 2:
                    return flat.rearrange("p (a b) -> p a b", a=shape[0])
                return flat.rearrange("p (a b c) -> p a b c", a=shape[0], b=shape[1])
            return carve

        carve = carver()
        dseg, tseg = carve(SL + 2).bitcast(I32), carve(SL).bitcast(I32)
        same, oh, fwd, bwd, cont = carve(SL + 1), carve(SL), carve(SL), carve(SL), carve(SL)
        sums = (cont[0:SEG, :], same[0:SEG, 0:SL])
        assert 4 * 4 * D <= 2 * SL
        last_row = work[0:96, 0:TLAST].bitcast(I32)
        e_cols = same[:, 0:3 * EP].bitcast(I32).rearrange("p (k c) -> p k c", k=3)
        rank_int = same[:, 3 * EP:4 * EP].bitcast(I32)
        e_dst, e_at, e_rel, part, rank = (same[:, k * EP:(k + 1) * EP] for k in range(4, 9))
        d_row, along_row, before, less = oh.bitcast(I32), fwd, bwd, cont
        carve = carver()
        xg = carve(4, 4 * D).rearrange("p b (j d) -> p b j d", j=4)
        zg = carve(2, 4, D)
        xt = carve(2, G)
        xe, ae = carve(4, D), carve(4, D)
        tri_inv, smat = carve(2, P), carve(2, P)
        xet, hpre, he, het = carve(2, D), carve(2, D), carve(2, D), carve(2, D)
        prod, msg, ao = carve(2, 4 * D), carve(2, D), carve(2, D)
        a1l, a2l, ze, xa = carve(4, D), carve(4, D), carve(4, D), carve(4, D)

        psum = ctx.enter_context(nc.psum_tensor("psum", [P, 8, 512], F32))
        AG, HT, ZB, WG, EB = 1, (2, 3), 4, 5, 7
        XT = ((0, EB), (0, 0))
        CT1, CM1, CT2, CM2 = (0, 1), (2, 3), (4, 7), (5, 6)
        XTE, AGG = psum[:, EB, 0:D], psum[:, AG, 0:D]

        ld_const, ld_edge, ld_seg, ld_w = (sem(s) for s in ("ld_const", "ld_edge", "ld_seg", "ld_w"))
        ld_trow, ld_last_row, last_onehot = sems("ld_trow", 2), sem("ld_last_row"), sem("last_onehot")
        prep = sem("prep")
        ends_out, ends_in, carry_out, carry_in = (sem(s) for s in (
            "ends_out", "ends_in", "carry_out", "carry_in"))
        ends_ready, carry_ready, memsets = sem("ends_ready"), sem("carry_ready"), sem("memsets")
        sums_ready, rows_ready, lin_out, ltile_in = (sem(s) for s in (
            "sums_ready", "rows_ready", "lin_out", "ltile_in"))
        ltr_ready, tables_ready, onehot_ready, w_ready, scan_ready = (sem(s) for s in (
            "ltr_ready", "tables_ready", "onehot_ready", "w_ready", "scan_ready"))
        descents_ready, descents_summed, order_known, order_ready = (
            sem(s) for s in ("descents_ready", "descents_summed", "order_known", "order_ready"))
        typ_copied, sort_in, piece_in, ranked = (
            sem(s) for s in ("typ_copied", "sort_in", "piece_in", "ranked"))
        blanked, placed, reloaded = sem("blanked"), sem("placed"), sem("reloaded")
        fill_set, fill_out = sem("fill_set"), sem("fill_out")
        ltile_set = sem("ltile_set")
        x_in = sems("x_in", 4)
        y_out = sems("y_out", 2)
        xt_done, xt_copied, xt_split, h_done, h_copied, h_split, z_done, z_added, sd_done, nb_done, y_done = (
            sem(s) for s in ("xt_done", "xt_copied", "xt_split", "h_done", "h_copied", "h_split", "z_done", "z_added",
                             "sd_done", "nb_done", "y_done"))
        stats_done, aggr_done, rs_done = sem("stats_done"), sem("aggr_done"), sem("rs_done")

        class Edge:

            def __init__(self, ph):
                self.x_in = sems(f"{ph}_x_in", 4)
                self.a_in = sems(f"{ph}_a_in", 4) if ph == "b" else None
                self.tri = sem(f"{ph}_tri")
                self.smat = sem(f"{ph}_smat")
                self.wg = sem(f"{ph}_wg")
                self.xet = sem(f"{ph}_xet")
                self.xetc = sem(f"{ph}_xetc")
                self.mm = sem(f"{ph}_mm")
                self.hpre = sem(f"{ph}_hpre")
                self.prod = sem(f"{ph}_prod")
                self.red = sem(f"{ph}_red")
                self.carry = sem(f"{ph}_carry")
                self.agg = sem(f"{ph}_agg")
                self.aggc = sem(f"{ph}_aggc")
                self.out = sems(f"{ph}_out", 2)
                self.ixc = sem(f"{ph}_ixc")

        ea, eb = Edge("a"), Edge("b")
        slot_out = sems("slot_out", 4)
        slot_in = sems("slot_in", 4)
        c_x_in, c_a_in, c_y_out = sems("c_x_in", 4), sems("c_a_in", 4), sems("c_y_out", 4)
        (c_ixc, c_ixs, c_t1, c_t1c, c_m1, c_hp, c_h, c_t2, c_t2c, c_m2, c_xa, c_z, c_st, c_mv, c_sd, c_rs,
         c_nb, c_y) = (sem(f"c_{s}") for s in (
             "ixc", "ixs", "t1", "t1c", "m1", "hp", "h", "t2", "t2c", "m2", "xa", "z", "st", "mv", "sd",
             "rs", "nb", "y"))

        LD_CONST = 12 * 16

        def col(tensor, n):
            return tensor[:, bass.ds(n, 1)]

        def rows(table, n):
            return table[bass.ds(n * P, P), :]

        def group(table, g):
            return table[bass.ds(g * G, G), :].rearrange("(p j) d -> p j d", j=4)

        def tail(table):
            return table[NG * G:N, :].rearrange("(p j) d -> p j d", j=4)

        block = ctx.enter_context(nc.Block())

        @block.sync
        def _(sp):
            for dst_ap, src_ap in ((tri_sb[:, :], tri), (iota_sb[:, :], iota), (ppos_sb[:, :], ppos),
                                   (rel_sb[:, :], rel), (sel_sb[:, :], sel), (ident_sb[:, :], ident),
                                   (anti_sb[:, :], anti),
                                   (root1_sb[:, :, :], root1.rearrange("(k p) n -> p k n", p=P)),
                                   (root2_sb[:, :, :], root2.rearrange("(k p) n -> p k n", p=P)),
                                   (first_carry[1:2, 0, :], b2[0:1, :]),
                                   (bias_row[:, :], b2.rearrange("l d -> (l d)").rearrange(
                                       "(o k) -> o k", o=1).broadcast_to([3, 2 * D])),
                                   (first_carry[1:2, 1, :], b2[1:2, :])):
                sp.dma_start(dst_ap, src_ap).then_inc(ld_const, 16)
            for s in range(SEG):
                sp.dma_start(dseg[16 * s:16 * s + 16, :],
                             dstseg[s:s + 1, :].broadcast_to([16, SL + 2])).then_inc(ld_seg, 16)
                sp.dma_start(tseg[16 * s:16 * s + 16, :],
                             typseg[s:s + 1, :].broadcast_to([16, SL])).then_inc(ld_seg, 16)
            sp.dma_start(src_sb[:, :], src).then_inc(ld_edge, 16)
            sp.dma_start(dst_sb[:, :], dst).then_inc(ld_edge, 16)
            sp.dma_start(slotid_sb[:, :], slotid).then_inc(ld_edge, 16)
            sp.dma_start(typ_slots, typ).then_inc(typ_copied, 16)
            sp.wait_ge(memsets, 1)
            for k in range(3):
                sp.dma_start(wf[32 * k:32 * k + 16, :], w1).then_inc(ld_w, 16)
            sp.wait_ge(fill_set, 1)
            sp.dma_start(node_slot.rearrange("(p k) o -> p (k o)", p=80), fill[:, :]).then_inc(fill_out, 16)
            sp.wait_ge(ends_ready, 1)
            sp.dma_start(seg_ends, ends[:, :]).then_inc(ends_out, 16)
            sp.wait_ge(ends_out, 16)
            sp.dma_start(ends_r[:, :, :], seg_ends.rearrange("(s r) q -> r s q", r=R)).then_inc(ends_in, 16)
            sp.wait_ge(carry_ready, 1)
            sp.dma_start(seg_carry.rearrange("(s r) q -> r s q", r=R), carry_r[:, :, :]).then_inc(carry_out, 16)
            sp.wait_ge(carry_out, 16)
            sp.dma_start(carry[:, :], seg_carry).then_inc(carry_in, 16)
            sp.wait_ge(w_ready, 1)
            for k in range(3):
                sp.dma_start(wf[32 * k:32 * k + 16, :], w2).then_inc(ld_w, 16)
            for t in range(2):
                lin = (lin_len, lin_count)[t]
                sp.dma_start(lin[E:LIN].rearrange("(o k) -> o k", o=1), pad_one[:, :]).then_inc(lin_out, 16)
            for t in range(2):
                sp.wait_ge(rows_ready, t + 1)
                lin = (lin_len, lin_count)[t]
                sp.dma_start(lin[0:E].rearrange("(s k) -> s k", s=SEG), sums[t]).then_inc(lin_out, 16)
            sp.wait_ge(lin_out, 64)
            sp.wait_ge(ltile_set, 1)
            for t in range(2):
                lin = (lin_len, lin_count)[t]
                for h, (c0, m) in enumerate(((0, P), (P, NCH - P))):
                    sp.dma_start(ltile[0:m, 2 * t + h, 2:P],
                                 lin[EC * c0:EC * (c0 + m)].rearrange("(c k) -> c k", k=EC)).then_inc(ltile_in, 16)
                    if t == 0:
                        sp.dma_start(ltile[0:m, h, 0:1],
                                     lin[EC * (c0 + 1):EC * (c0 + 1 + m)].rearrange("(c k) -> c k", k=EC)[:, 0:1],
                                     allow_slow_non_contiguous=True).then_inc(ltile_in, 16)

            def agg_store(e, table, n):
                sp.wait_ge(e.aggc, n.times(1, 1))
                sp.dma_start(rows(table, n.n), ao[:, n.at % 2, :]).then_inc(e.out[n.at % 2], 16)

            def y_store(g, m=P):
                sp.wait_ge(y_done, g.times(1, 1))
                sp.dma_start(group(y, g.n) if m == P else tail(y), zg[0:m, g.at % 2]).then_inc(y_out[g.at % 2], 16)

            def x_load(g, m=P):
                if g.at >= 4:
                    sp.wait_ge(z_added, g.times(2, -6))
                sp.dma_start(xg[0:m, g.at % 4], group(x, g.n) if m == P else tail(x)).then_inc(x_in[g.at % 4], 16)

            def step(e, table, n, g):
                if g is not None and not past(g.plus(3)):
                    x_load(g.plus(3), size(g.plus(3)))
                if n.at > 0:
                    agg_store(e, table, n.plus(-1))
                agg_store(e, table, n)
                if g is not None:
                    y_store(g, size(g))

            sp.wait_ge(last_onehot, 1)
            for u in range(3):
                x_load(Idx(u))
            phase_a(sp, lambda n, g: step(ea, agg1, n, g))
            agg_store(ea, agg1, Idx(NCH - 1))
            phase_b(sp, lambda n, g: step(eb, agg2, n, g))
            agg_store(eb, agg2, Idx(NCH - 1))
            sp.wait_ge(ea.out[0], 8 * NCH)
            sp.wait_ge(ea.out[1], 8 * NCH)
            sp.wait_ge(eb.out[0], 8 * NCH)
            sp.wait_ge(eb.out[1], 8 * NCH)

            def c_loads(n):
                r = n.at % 4
                if n.at >= 4:
                    sp.wait_ge(c_z, n.times(1, -3))
                sp.dma_start(a1l[:, r, :], rows(agg1, n.n)).then_inc(c_a_in[r], 16)
                sp.dma_start(a2l[:, r, :], rows(agg2, n.n)).then_inc(c_a_in[r], 16)

            for k in range(C_PRO):
                c_loads(Idx(k))
            with sp.Fori(0, C_IT) as i:
                for u in range(4):
                    c_loads(Idx(C_PRO + u, i))
            sp.wait_ge(y_out[0], 16 * ((NG + 2) // 2))
            sp.wait_ge(y_out[1], 16 * ((NG + 1) // 2))
            for r in range(4):
                sp.wait_ge(c_y_out[r], 4 * NCH)

        @block.gpsimd
        def _(pool):
            nc.gpsimd.memset(fill[:, :], 1).then_inc(fill_set, 1)

            def sort_edges():
                for out_ap, in_ap in ((e_cols, edges), (e_at, eidx),
                                      (along_row, along.broadcast_to([P, SL]))):
                    pool.dma_start(out_ap, in_ap).then_inc(sort_in, 16)
                for s in range(SEG):
                    if s:
                        pool.wait_ge(ranked, s)
                    pool.dma_start(d_row, dstseg[s:s + 1, 1:SL + 1].broadcast_to([P, SL])).then_inc(piece_in, 16)
                for table, row in ((dst_lin, 0), (typ_lin, 1), (src_lin, 1)):
                    pool.dma_start(table.rearrange("k o -> o k"), blank[row:row + 1, :]).then_inc(blanked, 16)
                pool.wait_ge(blanked, 48)
                pool.wait_ge(ranked, SEG + 1)
                last_edge = nc.gpsimd.to_reg(E)

                def place(c):
                    nc.gpsimd.tensor_copy(rank_ix[:, :], rank_int[:, bass.ds(c, 1)])
                    for k in range(3):
                        nc.gpsimd.tensor_copy(rec_ix[:, k:k + 1], e_cols[:, k, bass.ds(c, 1)])
                    pool.drain()
                    for k, table in enumerate((dst_lin, typ_lin, src_lin)):
                        nc.gpsimd.indirect_dma_start(
                            table, bass.IndirectOffsetOnAxis(ap=rank_ix[:, 0:1], axis=0), rec_ix[:, k:k + 1], None,
                            bounds_check=last_edge, oob_is_err=False).then_inc(placed, 16)

                place(0)
                with pool.Fori(0, EP - 1) as i:
                    pool.wait_ge(placed, i * 48 + 48)
                    place(i + 1)
                pool.wait_ge(placed, 48 * EP)
                pool.wait_ge(ld_edge, 48)
                pool.wait_ge(typ_copied, 16)
                for s in range(SEG):
                    pool.dma_start(dseg[16 * s:16 * s + 16, :], dst_lin[s * SL:s * SL + SL + 2, :].rearrange(
                        "k o -> o k").broadcast_to([16, SL + 2])).then_inc(reloaded, 16)
                    pool.dma_start(tseg[16 * s:16 * s + 16, :], typ_lin[1 + s * SL:1 + s * SL + SL, :].rearrange(
                        "k o -> o k").broadcast_to([16, SL])).then_inc(reloaded, 16)
                for n in range(NCH):
                    at = 1 + EC * (NCH - 1 - n)
                    for by_slot, table in ((dst_sb[2:P, n:n + 1], dst_lin), (src_sb[2:P, n:n + 1], src_lin),
                                           (typ_slots[n, 2:P].rearrange("(k o) -> k o", o=1), typ_lin)):
                        pool.dma_start(by_slot, table[at:at + EC, :]).then_inc(reloaded, 16)
                pool.wait_ge(reloaded, 16 * (2 * SEG + 3 * NCH))

            pool.wait_ge(order_known, 1)
            disorder = nc.gpsimd.value_load(unsorted[0:1, 0:1], min_val=0, max_val=1)
            with pool.If(disorder > 0):
                sort_edges()
            nc.gpsimd.memset(rank_ix[:, :], 0).then_inc(order_ready, 1)
            for k in range(TROWS):
                pool.wait_ge(ld_trow[k % 2], 16 * (k // 2 + 1))
                nc.gpsimd.tensor_scalar(onehot[:, k * TROW:(k + 1) * TROW], trow[:, k % 2, :], rel_sb[0:96, 1:2],
                                        None, ALU.is_equal).then_inc(onehot_ready, 1)
            pool.wait_ge(ld_edge, 48)
            pool.wait_ge(tables_ready, 1)
            pool.wait_ge(fill_out, 16)

            def column(n, kind, table, done):
                nc.gpsimd.tensor_copy(ix[:, kind, n.at % 4:n.at % 4 + 1], col(table, n.n)).then_inc(done, 1)

            last_node = nc.gpsimd.to_reg(N - 1)

            def gather(out_ap, table, index_ap, done):
                nc.gpsimd.indirect_dma_start(
                    out_ap, None, table, bass.IndirectOffsetOnAxis(ap=index_ap, axis=0),
                    bounds_check=last_node, oob_is_err=False).then_inc(done, 16)

            def scatter(table, index_ap, in_ap, done):
                nc.gpsimd.indirect_dma_start(
                    table, bass.IndirectOffsetOnAxis(ap=index_ap, axis=0), in_ap, None,
                    bounds_check=last_node, oob_is_err=False).then_inc(done, 16)

            def low_x(g, k, m=P):
                pool.wait_ge(xt_copied, g.times(2, 1 + k))
                nc.gpsimd.tensor_tensor(xt_lo[:, k, 0:4 * m], xt[:, k, 0:4 * m],
                                        xt_hi[:, k, 0:4 * m].bitcast(F32), ALU.subtract).then_inc(xt_split, 1)

            def step(chunk, lead, n, g):
                if g is not None and not past(g.plus(2)):
                    low_x(g.plus(2), 0, size(g.plus(2)))
                    low_x(g.plus(2), 1, size(g.plus(2)))
                chunk(n.plus(lead))
                chunk(n.plus(lead + 1))

            def a_columns(n):
                column(n, 0, src_sb, ea.ixc)
                column(n, 1, first_dst, ea.ixc)
                column(n, 2, slotid_sb, ea.ixc)

            def a_chunk(n):
                r, ahead = n.at % 4, n.plus(1)
                if past_chunks(n):
                    return
                if n.at >= 4:
                    pool.wait_ge(ea.prod, n.times(1, -3))
                if ahead.at >= 4:
                    pool.wait_ge(ea.x_in[ahead.at % 4], ahead.used(4))
                    pool.wait_ge(slot_out[ahead.at % 4], ahead.used(4))
                pool.wait_ge(ea.ixc, n.times(3, 3))
                if not past_chunks(ahead):
                    a_columns(ahead)
                gather(xe[:, r, :], x, ix[:, 0, r:r + 1], ea.x_in[r])
                scatter(node_slot, ix[:, 1, r:r + 1], ix[:, 2, r:r + 1], slot_out[r])

            a_columns(Idx(0))
            a_chunk(Idx(0))
            low_x(Idx(0), 0)
            low_x(Idx(0), 1)
            for k in range(1, A_LEAD):
                a_chunk(Idx(k))
            low_x(Idx(1), 0)
            low_x(Idx(1), 1)
            phase_a(pool, lambda n, g: step(a_chunk, A_LEAD, n, g))

            for r in range(4):
                pool.wait_ge(slot_out[r], 4 * NCH)
                pool.wait_ge(ea.x_in[r], 4 * NCH)
            pool.wait_ge(ea.prod, NCH)

            def b_chunk(n):
                r, ahead, back = n.at % 4, n.plus(1), n.plus(-1)
                q = back.at % 4
                if past_chunks(back):
                    return
                if n.at >= 4 and not past_chunks(n):
                    pool.wait_ge(eb.prod, n.times(1, -3))
                    pool.wait_ge(eb.a_in[r], n.used(4))
                if ahead.at >= 4 and not past_chunks(ahead):
                    pool.wait_ge(eb.x_in[ahead.at % 4], ahead.used(4))
                    pool.wait_ge(slot_in[ahead.at % 4], ahead.used(4))
                if not past_chunks(n):
                    pool.wait_ge(eb.ixc, n.times(1, 1))
                if back.at >= 0:
                    pool.wait_ge(slot_in[q], back.inn(4))
                if back.at >= 4:
                    pool.wait_ge(eb.hpre, back.times(1, -3))
                if not past_chunks(ahead):
                    column(ahead, 0, src_sb, eb.ixc)
                if not past_chunks(n):
                    gather(slot_ix[:, r:r + 1], node_slot, ix[:, 0, r:r + 1], slot_in[r])
                    gather(xe[:, r, :], x, ix[:, 0, r:r + 1], eb.x_in[r])
                if back.at == 0:
                    pool.wait_ge(ea.out[0], 8 * NCH)
                    pool.wait_ge(ea.out[1], 8 * NCH)
                if back.at >= 0:
                    gather(ae[:, q, :], agg1, slot_ix[:, q:q + 1], eb.a_in[q])

            column(Idx(0), 0, src_sb, eb.ixc)
            for k in range(B_LEAD):
                b_chunk(Idx(k))
            phase_b(pool, lambda n, g: step(b_chunk, B_LEAD, n, g))

            pool.wait_ge(eb.prod, NCH)
            for r in range(4):
                pool.wait_ge(eb.x_in[r], 4 * NCH)

            def c_chunk(n):
                r, ahead, back = n.at % 4, n.plus(1), n.plus(-C_LEAD)
                q, back1 = back.at % 4, back.plus(1)
                if n.at >= 4 and not past_chunks(n):
                    pool.wait_ge(c_xa, n.times(1, -3))
                    pool.wait_ge(c_t1, n.times(1, -3))
                if ahead.at >= 4 and not past_chunks(ahead):
                    pool.wait_ge(c_x_in[ahead.at % 4], ahead.used(4))
                if back1.at >= 4 and not past_chunks(back1):
                    pool.wait_ge(c_y_out[back1.at % 4], back1.used(4))
                if not past_chunks(n):
                    pool.wait_ge(c_ixc, n.times(1, 1))
                if back.at == 0:
                    pool.wait_ge(y_out[0], 16 * ((NG + 2) // 2))
                    pool.wait_ge(y_out[1], 16 * ((NG + 1) // 2))
                if back.at >= 0:
                    pool.wait_ge(c_ixs, back.times(1, 1))
                    pool.wait_ge(c_y, back.times(1, 1))
                if not past_chunks(ahead):
                    column(ahead, 0, first_dst, c_ixc)
                if back1.at >= 0 and not past_chunks(back1):
                    column(back1, 1, first_dst, c_ixs)
                if back.at >= 0:
                    scatter(y, ix[:, 1, q:q + 1], ze[:, q, :], c_y_out[q])
                if not past_chunks(n):
                    gather(xe[:, r, :], x, ix[:, 0, r:r + 1], c_x_in[r])

            column(Idx(0), 0, first_dst, c_ixc)
            for k in range(12):
                c_chunk(Idx(k))
            with pool.Fori(0, C_IT - 1) as i:
                for u in range(4):
                    c_chunk(Idx(12 + u, i))
            for k in range(NCH - 4, NCH + C_LEAD):
                c_chunk(Idx(k))

        @block.scalar
        def _(act):
            def relu(g, j, m=P):
                if g.at > 0 and j == 0:
                    act.wait_ge(z_done, g.times(2))
                act.wait_ge(h_done, g.times(2, 1 + j))
                nc.scalar.activation(ht_hi[:, j, 0:4 * m], psum[:, HT[j], 0:4 * m],
                                     ACT.Relu).then_inc(h_copied, 1)

            def xt_copy(g, k, layer, m=P):
                if g.at > 0 and k == 0:
                    act.wait_ge(h_done, g.times(2))
                act.wait_ge(xt_done, g.times(2, 1 + k))
                nc.scalar.copy(xt[:, k, 0:4 * m], psum[:, XT[layer][k], 0:4 * m])
                nc.scalar.copy(xt_hi[:, k, 0:4 * m], psum[:, XT[layer][k], 0:4 * m]).then_inc(xt_copied, 1)

            def deviation(g, m=P):
                act.wait_ge(aggr_done, g.times(4, 4))
                nc.scalar.activation(sd_d[0:m, :], mv_d[0:m, :, 1], ACT.Sqrt,
                                     bias=eps_col[0:m, :]).then_inc(sd_done, 1)

            def normalise(g, m=P):
                act.wait_ge(nb_done, g.times(1, 1))
                for t in range(4):
                    last = nc.scalar.activation(zg[0:m, g.at % 2, t, :], zg[0:m, g.at % 2, t, :],
                                                ACT.Identity, bias=nb_d[0:m, t:t + 1], scale=rs_d[0:m, t:t + 1])
                last.then_inc(y_done, 1)

            def scaled_triangle(e, n):
                if n.at >= 2:
                    act.wait_ge(e.smat, n.times(1, -1))
                nc.scalar.activation(tri_inv[:, n.at % 2, :], tri_sb[:, :], ACT.Copy,
                                     scale=col(inv_sb, n.n)).then_inc(e.tri, 1)

            def rows_t_copy(n):
                act.wait_ge(eb.xet, n.times(1, 1))
                if n.at >= 2:
                    act.wait_ge(eb.mm, n.times(1, -1))
                nc.scalar.copy(xet[:, n.at % 2, :], XTE).then_inc(eb.xetc, 1)

            def aggregate_copy(e, n):
                act.wait_ge(e.agg, n.times(1, 1))
                if n.at >= 2:
                    act.wait_ge(e.out[n.at % 2], n.used(2))
                    act.wait_ge(e.carry, n.n)
                nc.scalar.copy(ao[:, n.at % 2, :], AGG).then_inc(e.aggc, 1)

            def carry_rows(e, layer, n):
                act.wait_ge(e.red, n.times(1, 1))
                if n.at == 0:
                    source = first_carry[:, layer, :]
                else:
                    act.wait_ge(e.aggc, n.n)
                    source = ao[0:2, (n.at - 1) % 2, :]
                nc.scalar.copy(msg[0:2, n.at % 2, :], source).then_inc(e.carry, 1)

            def step(e, layer, n, g):
                n2, n3 = n.plus(1), n.plus(2)
                more = g is not None and not past(g.plus(1))
                more2 = g is not None and not past(g.plus(2))
                scaled_triangle(e, n2)
                if more:
                    relu(g.plus(1), 0, size(g.plus(1)))
                carry_rows(e, layer, n)
                if layer:
                    rows_t_copy(n2)
                if more:
                    relu(g.plus(1), 1, size(g.plus(1)))
                aggregate_copy(e, n)
                if g is not None:
                    deviation(g, size(g))
                if more2:
                    xt_copy(g.plus(2), 0, layer, size(g.plus(2)))
                if more2 and not layer:
                    xt_copy(g.plus(2), 1, layer, size(g.plus(2)))
                if not past_chunks(n3):
                    scaled_triangle(e, n3)
                    if layer:
                        rows_t_copy(n3)
                if more2 and layer:
                    xt_copy(g.plus(2), 1, layer, size(g.plus(2)))
                carry_rows(e, layer, n2)
                aggregate_copy(e, n2)
                if g is not None:
                    normalise(g, size(g))

            act.wait_ge(typ_copied, 16)
            act.wait_ge(order_ready, 1)
            typ_row = typ_slots.rearrange("c (o p) -> o (c p)", o=1)
            for k in range(TROWS):
                if k >= 2:
                    act.wait_ge(onehot_ready, k - 1)
                act.dma_start(trow[:, k % 2, :], typ_row[0:1, k * TROW:(k + 1) * TROW].broadcast_to(
                    [96, TROW])).then_inc(ld_trow[k % 2], 16)
                if k == TROWS // 2:
                    act.wait_ge(ends_ready, 1)
                    act.dma_start(last_row, typ_row[0:1, TROWS * TROW:SLOTS].broadcast_to(
                        [96, TLAST])).then_inc(ld_last_row, 16)
            act.wait_ge(ld_const, LD_CONST)
            act.wait_ge(memsets, 1)
            act.wait_ge(tables_ready, 1)
            xt_copy(Idx(0), 0, 0)
            xt_copy(Idx(0), 1, 0)
            relu(Idx(0), 0)
            relu(Idx(0), 1)
            xt_copy(Idx(1), 0, 0)
            xt_copy(Idx(1), 1, 0)
            scaled_triangle(ea, Idx(0))
            phase_a(act, lambda n, g: step(ea, 0, n, g))
            act.wait_ge(ea.out[0], 8 * NCH)
            act.wait_ge(ea.out[1], 8 * NCH)
            scaled_triangle(eb, Idx(0))
            rows_t_copy(Idx(0))
            phase_b(act, lambda n, g: step(eb, 1, n, g))

            def c_t1_copy(n):
                act.wait_ge(c_t1, n.times(1, 1))
                if n.at >= 2:
                    act.wait_ge(c_m1, n.times(1, -1))
                nc.scalar.copy(xet[:, n.at % 2, :], psum[:, CT1[n.at % 2], 0:D]).then_inc(c_t1c, 1)

            def c_relu(n):
                act.wait_ge(c_hp, n.times(1, 1))
                if n.at >= 2:
                    act.wait_ge(c_t2, n.times(1, -1))
                nc.scalar.activation(he[:, n.at % 2, :], hpre[:, n.at % 2, :], ACT.Relu).then_inc(c_h, 1)

            def c_t2_copy(n):
                act.wait_ge(c_t2, n.times(1, 1))
                if n.at >= 2:
                    act.wait_ge(c_m2, n.times(1, -1))
                nc.scalar.copy(het[:, n.at % 2, :], psum[:, CT2[n.at % 2], 0:D]).then_inc(c_t2c, 1)

            def c_deviation(n):
                b = n.at % 2
                act.wait_ge(c_mv, n.times(1, 1))
                nc.scalar.activation(sd_e[:, b:b + 1], mv_e[:, b, 1:2], ACT.Sqrt,
                                     bias=eps_col[:, :]).then_inc(c_sd, 1)

            def c_normalise(n):
                b, r = n.at % 2, n.at % 4
                act.wait_ge(c_nb, n.times(1, 1))
                nc.scalar.activation(ze[:, r, :], ze[:, r, :], ACT.Identity, bias=nb_e[:, b:b + 1],
                                     scale=rs_e[:, b:b + 1]).then_inc(c_y, 1)

            c_slots(act, ((4, c_normalise), (2, c_t2_copy), (1, c_relu), (3, c_deviation), (0, c_t1_copy)))

        @block.vector
        def _(dve):
            steps = [0]

            def link(ins):
                steps[0] += 1
                ins.then_inc(prep, 1)
                dve.wait_ge(prep, steps[0])

            nc.vector.memset(eps_col[:, :], EPS)
            nc.vector.memset(ones3[:, :], 1.0)
            nc.vector.memset(pad_one[:, :], 1.0)
            nc.vector.memset(first_carry[0:1, :, :], 0.0)
            nc.vector.memset(wcat[:, :, :], 0.0)
            nc.vector.memset(wf[:, :], 0.0).then_inc(memsets, 1)
            nc.vector.memset(ltile[:, 0:2, 1:2], 1.0)
            nc.vector.memset(ltile[:, 2:4, 0:2], 1.0).then_inc(ltile_set, 1)

            def split_w(layer):
                dve.wait_ge(memsets, 1)
                dve.wait_ge(ld_w, 48 * (layer + 1))
                nc.vector.tensor_copy(wcat[0:16, layer, :], wf[0:16, :])
                for k in (1, 2):
                    p = slice(32 * k, 32 * k + 16)
                    link(nc.vector.tensor_copy(wcat[p, layer, :], wf[p, :]))
                    for _ in range(k - 1):
                        link(nc.vector.tensor_tensor(wf[p, :], wf[p, :], wcat[p, layer, :], ALU.subtract))
                        link(nc.vector.tensor_copy(wcat[p, layer, :], wf[p, :]))
                    link(nc.vector.tensor_tensor(wf[p, :], wf[p, :], wcat[p, layer, :], ALU.subtract))
                    last = nc.vector.tensor_copy(wcat[p, layer, :], wf[p, :])
                last.then_inc(w_ready, 1)
                dve.wait_ge(w_ready, layer + 1)

            dve.wait_ge(ld_seg, 256)
            dve.wait_ge(ld_const, LD_CONST)
            link(nc.vector.memset(ones_col[:, :], 1.0))
            link(nc.vector.tensor_tensor(same[:, :], dseg[:, 1:SL + 2], dseg[:, 0:SL + 1], ALU.is_lt))
            nc.vector.tensor_reduce(descents[:, :], same[:, :], AX.X, ALU.max).then_inc(descents_ready, 1)
            dve.wait_ge(descents_summed, 1)
            nc.vector.tensor_scalar(unsorted[:, :], psum[0:1, AG, 0:1], 0.5, None, ALU.is_gt).then_inc(order_known, 1)
            dve.wait_ge(order_known, 1)

            def rank_edges():
                dve.wait_ge(sort_in, 48)
                nc.vector.tensor_copy(e_dst, e_cols[:, 0, :])
                nc.vector.memset(rank, 1.0)
                dve.drain()
                for s in range(SEG):
                    nc.vector.tensor_scalar(e_rel, e_at, float(-s * SL), None, ALU.add)
                    dve.wait_ge(piece_in, 16 * (s + 1))
                    dve.drain()
                    with dve.Fori(0, EP) as c:
                        one = bass.ds(c, 1)
                        nc.vector.scalar_tensor_tensor(before, along_row, e_rel[:, one], along_row, ALU.is_lt,
                                                       ALU.bypass)
                        dve.drain()
                        nc.vector.scalar_tensor_tensor(less, d_row, e_dst[:, one], before, ALU.is_equal, ALU.mult)
                        dve.drain()
                        nc.vector.scalar_tensor_tensor(before, d_row, e_dst[:, one], less, ALU.is_lt, ALU.add)
                        dve.drain()
                        nc.vector.tensor_reduce(part[:, one], before, AX.X, ALU.add)
                        dve.drain()
                    nc.vector.tensor_tensor(rank, rank, part, ALU.add).then_inc(ranked, 1)
                    dve.drain()
                nc.vector.tensor_copy(rank_int, rank).then_inc(ranked, 1)
                dve.wait_ge(reloaded, 16 * (2 * SEG + 3 * NCH))

            disorder = nc.vector.value_load(unsorted[0:1, 0:1], min_val=0, max_val=1)
            with dve.If(disorder > 0):
                rank_edges()
            link(nc.vector.tensor_tensor(same[:, :], dseg[:, 0:SL + 1], dseg[:, 1:SL + 2], ALU.is_equal))
            link(nc.vector.tensor_scalar(oh[:, :], tseg[:, :], rel_sb[:, 0:1], None, ALU.is_equal))
            into, onto = same[:, 0:SL], same[:, 1:SL + 1]
            link(nc.vector.tensor_tensor_scan(fwd[:, :], into, oh[:, :], 0.0, ALU.mult, ALU.add))
            link(nc.vector.tensor_tensor_scan(bwd[:, ::-1], onto[:, ::-1], oh[:, ::-1], 0.0, ALU.mult, ALU.add))
            link(nc.vector.tensor_copy(ends[:, 0:1], fwd[:, SL - 1:SL]))
            link(nc.vector.tensor_copy(ends[:, 2:3], bwd[:, 0:1]))
            link(nc.vector.tensor_reduce(ends[:, 1:2], into, AX.X, ALU.min))
            nc.vector.tensor_reduce(ends[:, 3:4], onto, AX.X, ALU.min).then_inc(ends_ready, 1)
            split_w(0)
            dve.wait_ge(ends_in, 16)
            link(nc.vector.memset(carry_r[:, 0:1, 0:1], 0.0))
            link(nc.vector.memset(carry_r[:, SEG - 1:SEG, 1:2], 0.0))
            link(nc.vector.tensor_tensor_scan(carry_r[:, 1:SEG, 0], ends_r[:, 0:SEG - 1, 1],
                                              ends_r[:, 0:SEG - 1, 0], 0.0, ALU.mult, ALU.add))
            nc.vector.tensor_tensor_scan(carry_r[:, 0:SEG - 1, 1][:, ::-1], ends_r[:, 1:SEG, 3][:, ::-1],
                                         ends_r[:, 1:SEG, 2][:, ::-1], 0.0, ALU.mult, ALU.add).then_inc(carry_ready, 1)
            link(nc.vector.tensor_tensor_scan(cont[:, :], into, into, 1.0, ALU.mult, ALU.min))
            dve.wait_ge(carry_in, 16)
            link(nc.vector.scalar_tensor_tensor(fwd[:, :], cont[:, :], carry[:, 0:1], fwd[:, :], ALU.mult, ALU.add))
            link(nc.vector.tensor_tensor_scan(cont[:, ::-1], onto[:, ::-1], onto[:, ::-1], 1.0, ALU.mult, ALU.min))
            link(nc.vector.scalar_tensor_tensor(bwd[:, :], cont[:, :], carry[:, 1:2], bwd[:, :], ALU.mult, ALU.add))
            link(nc.vector.tensor_tensor(bwd[:, :], fwd[:, :], bwd[:, :], ALU.add))
            nc.vector.scalar_tensor_tensor(bwd[:, :], bwd[:, :], -1.0, oh[:, :], ALU.add, ALU.mult).then_inc(scan_ready, 1)
            split_w(1)
            dve.wait_ge(sums_ready, 1)
            for k in range(PIECES):
                m = min(512, SL - 512 * k)
                last = nc.vector.tensor_copy(sums[0][:, 512 * k:512 * k + m], psum[0:SEG, k, 0:m])
            last.then_inc(rows_ready, 1)
            dve.wait_ge(ld_last_row, 16)
            nc.vector.tensor_scalar(onehot[:, TROWS * TROW:SLOTS], last_row, rel_sb[0:96, 1:2], None,
                                    ALU.is_equal).then_inc(last_onehot, 1)
            dve.wait_ge(sums_ready, 2)
            for k in range(PIECES):
                m = min(512, SL - 512 * k)
                last = nc.vector.tensor_copy(sums[1][:, 512 * k:512 * k + m], psum[0:SEG, k, 0:m])
            last.then_inc(rows_ready, 1)
            link(nc.vector.tensor_copy(bias_parts[:, 0, :], bias_row[:, :]))
            link(nc.vector.tensor_tensor(bias_res[:, :], bias_row[:, :], bias_parts[:, 0, :], ALU.subtract))
            link(nc.vector.tensor_copy(bias_parts[:, 1, :], bias_res[:, :]))
            link(nc.vector.tensor_tensor(bias_res[:, :], bias_res[:, :], bias_parts[:, 1, :], ALU.subtract))
            link(nc.vector.tensor_copy(bias_parts[:, 2, :], bias_res[:, :]))
            link(nc.vector.tensor_scalar(bias_sel[:, :], bias_parts[:, 0, :], ident_sb[0:3, 0:1], None, ALU.mult))
            for k in (1, 2):
                link(nc.vector.scalar_tensor_tensor(bias_sel[:, :], bias_parts[:, k, :], ident_sb[0:3, k:k + 1],
                                                    bias_sel[:, :], ALU.mult, ALU.add))
            nc.vector.tensor_copy(b1_bf[:, :], bias_sel[:, 0:D])
            nc.vector.tensor_copy(b2_bf[:, 0, :], bias_sel[:, D:2 * D])
            nc.vector.tensor_copy(b2_bf[:, 1, :], bias_sel[:, D:2 * D])
            nc.vector.tensor_copy(root1_hi[:, :, :], root1_sb[:, :, :])
            link(nc.vector.tensor_copy(root2_hi[:, :, :], root2_sb[:, :, :]))
            nc.vector.tensor_tensor(root1_lo[:, :, :], root1_sb[:, :, :], root1_hi[:, :, :].bitcast(F32), ALU.subtract)
            nc.vector.tensor_tensor(root2_lo[:, :, :], root2_sb[:, :, :], root2_hi[:, :, :].bitcast(F32), ALU.subtract)
            dve.wait_ge(ltr_ready, 1)
            dve.wait_ge(ld_edge, 48)
            link(nc.vector.tensor_copy(len_sb[:, :], psum[:, 0, 0:NCH]))
            link(nc.vector.reciprocal(inv_sb[:, :], psum[:, 1, 0:NCH]))
            link(nc.vector.tensor_scalar(start_sb[:, :], len_sb[:, :], -1.0, ppos_sb[:, 0:1], ALU.mult, ALU.add))
            link(nc.vector.tensor_scalar(later[:, :], len_sb[:, :], 1.0, float(BIG), ALU.is_gt, ALU.mult))
            nc.vector.tensor_tensor(first_dst[:, :], dst_sb[:, :], later[:, :], ALU.add).then_inc(tables_ready, 1)

            def low_h(g, j, m=P):
                dve.wait_ge(h_copied, g.times(2, 1 + j))
                nc.vector.scalar_tensor_tensor(ht_lo[:, j, 0:4 * m], psum[:, HT[j], 0:4 * m], 0.0,
                                               ht_hi[:, j, 0:4 * m].bitcast(F32), ALU.max,
                                               ALU.subtract).then_inc(h_split, 1)

            def add_x(g, q, m=P):
                b = g.at % 2
                dve.wait_ge(z_done, g.times(2, 1 + q))
                if g.at >= 2 and q == 0:
                    dve.wait_ge(y_out[b], g.used(2))
                nc.vector.tensor_tensor(zg[0:m, b, 2 * q:2 * q + 2, :].rearrange("p t d -> p (t d)"),
                                        psum[0:m, ZB, :],
                                        xg[0:m, g.at % 4, 2 * q:2 * q + 2, :].rearrange("p t d -> p (t d)"),
                                        ALU.add).then_inc(z_added, 1)

            def statistics(g, q, m=P):
                b = g.at % 2
                dve.wait_ge(z_added, g.times(2, 1 + q))
                if g.at >= 1 and q == 0:
                    dve.wait_ge(aggr_done, g.times(4))
                for t in (2 * q, 2 * q + 1):
                    nc.vector.bn_stats(st_d[0:m, t, :], zg[0:m, b, t, :]).then_inc(stats_done, 1)

            def before_moments(g):
                dve.wait_ge(stats_done, g.times(4, 4))
                if g.at >= 1:
                    dve.wait_ge(nb_done, g.n)

            def moments(g, m=P):
                for t in range(4):
                    nc.vector.bn_aggr(mv_d[0:m, t, :], st_d[0:m, t, :]).then_inc(aggr_done, 1)

            def scales(g, m=P):
                dve.wait_ge(sd_done, g.times(1, 1))
                if g.at >= 1:
                    dve.wait_ge(y_done, g.n)
                nc.vector.reciprocal(rs_d[0:m, :], sd_d[0:m, :]).then_inc(rs_done, 1)
                dve.wait_ge(rs_done, g.times(1, 1))
                nc.vector.scalar_tensor_tensor(nb_d[0:m, :], mv_d[0:m, :, 0], -1.0, rs_d[0:m, :], ALU.mult,
                                               ALU.mult).then_inc(nb_done, 1)

            def suffix_matrix(e, n):
                b = n.at % 2
                dve.wait_ge(e.tri, n.times(1, 1))
                if n.at >= 2:
                    dve.wait_ge(e.agg, n.times(1, -1))
                nc.vector.scalar_tensor_tensor(smat[:, b, :], iota_sb[:, :], col(start_sb, n.n), tri_inv[:, b, :],
                                               ALU.is_ge, ALU.mult).then_inc(e.smat, 1)

            def messages(e, layer, n):
                b, r = n.at % 2, n.at % 4
                if layer:
                    dve.wait_ge(eb.a_in[r], n.inn(4))
                    dve.wait_ge(eb.mm, n.times(1, 1))
                    if n.at >= 2:
                        dve.wait_ge(eb.prod, n.times(1, -1))
                    nc.vector.tensor_tensor(hpre[:, b, :], XTE, ae[:, r, :], ALU.add).then_inc(eb.hpre, 1)
                    dve.wait_ge(eb.hpre, n.times(1, 1))
                    row, least = hpre[:, b, :], 0.0
                else:
                    dve.wait_ge(ea.x_in[r], n.inn(4))
                    row, least = xe[:, r, :], None
                dve.wait_ge(e.wg, n.times(1, 1))
                if n.at >= 2:
                    dve.wait_ge(e.red, n.times(1, -1))
                four = row.unsqueeze(1).broadcast_to([P, 4, D])
                out_ap = prod[:, b, :].rearrange("p (o k) -> p o k", o=4)
                w_ap = psum[:, WG:WG + 2, :].rearrange("p a (h k) -> p (a h) k", h=2)
                nc.vector.scalar_tensor_tensor(out_ap, four, 1.0 if least is None else least, w_ap,
                                               ALU.mult if least is None else ALU.max,
                                               ALU.mult).then_inc(e.prod, 1)

            def sum_messages(e, n):
                b = n.at % 2
                dve.wait_ge(e.prod, n.times(1, 1))
                nc.vector.tensor_reduce(msg[:, b, :].rearrange("p (b o) -> p o b", o=4),
                                        prod[:, b, :].rearrange("p (o b i) -> p o b i", o=4, i=4),
                                        AX.X, ALU.add).then_inc(e.red, 1)

            def step(e, layer, n, g):
                n2 = n.plus(1)
                more = g is not None and not past(g.plus(1))
                suffix_matrix(e, n)
                messages(e, layer, n)
                if g is not None:
                    add_x(g, 1, size(g))
                sum_messages(e, n)
                if g is not None:
                    statistics(g, 1, size(g))
                if more:
                    low_h(g.plus(1), 0, size(g.plus(1)))
                if g is not None:
                    before_moments(g)
                suffix_matrix(e, n2)
                if g is not None:
                    moments(g, size(g))
                if more:
                    low_h(g.plus(1), 1, size(g.plus(1)))
                messages(e, layer, n2)
                sum_messages(e, n2)
                if g is not None:
                    scales(g, size(g))
                if more:
                    add_x(g.plus(1), 0, size(g.plus(1)))
                    statistics(g.plus(1), 0, size(g.plus(1)))

            low_h(Idx(0), 0)
            low_h(Idx(0), 1)
            add_x(Idx(0), 0)
            statistics(Idx(0), 0)
            phase_a(dve, lambda n, g: step(ea, 0, n, g))
            dve.wait_ge(ea.agg, NCH)
            dve.wait_ge(ea.red, NCH)
            phase_b(dve, lambda n, g: step(eb, 1, n, g))
            dve.wait_ge(eb.prod, NCH)

            def c_add_agg1(n):
                b, r = n.at % 2, n.at % 4
                dve.wait_ge(c_m1, n.times(1, 1))
                dve.wait_ge(c_a_in[r], two(n))
                if n.at >= 2:
                    dve.wait_ge(c_h, n.times(1, -1))
                nc.vector.tensor_tensor(hpre[:, b, :], psum[:, CM1[b], 0:D], a1l[:, r, :], ALU.add).then_inc(c_hp, 1)

            def c_add_agg2(n):
                b = r = n.at % 4
                dve.wait_ge(c_a_in[r], two(n))
                dve.wait_ge(c_x_in[r], n.inn(4))
                if n.at >= 4:
                    dve.wait_ge(c_z, n.times(1, -3))
                nc.vector.tensor_tensor(xa[:, b, :], xe[:, r, :], a2l[:, r, :], ALU.add).then_inc(c_xa, 1)

            def c_statistics(n):
                b, r = n.at % 2, n.at % 4
                dve.wait_ge(c_m2, n.times(1, 1))
                dve.wait_ge(c_xa, n.times(1, 1))
                if n.at >= 4:
                    dve.wait_ge(c_y_out[r], n.used(4))
                nc.vector.tensor_tensor(ze[:, r, :], psum[:, CM2[b], 0:D], xa[:, r, :], ALU.add).then_inc(c_z, 1)
                dve.wait_ge(c_z, n.times(1, 1))
                if n.at >= 2:
                    dve.wait_ge(c_mv, n.times(1, -1))
                nc.vector.bn_stats(st_e[:, b, :], ze[:, r, :]).then_inc(c_st, 1)
                dve.wait_ge(c_st, n.times(1, 1))
                if n.at >= 2:
                    dve.wait_ge(c_nb, n.times(1, -1))

            def c_moments(n):
                b = n.at % 2
                nc.vector.bn_aggr(mv_e[:, b, :], st_e[:, b, :]).then_inc(c_mv, 1)

            def c_scale(n):
                b = n.at % 2
                dve.wait_ge(c_sd, n.times(1, 1))
                if n.at >= 2:
                    dve.wait_ge(c_y, n.times(1, -1))
                nc.vector.reciprocal(rs_e[:, b:b + 1], sd_e[:, b:b + 1]).then_inc(c_rs, 1)
                dve.wait_ge(c_rs, n.times(1, 1))
                nc.vector.scalar_tensor_tensor(nb_e[:, b:b + 1], mv_e[:, b, 0:1], -1.0, rs_e[:, b:b + 1], ALU.mult,
                                               ALU.mult).then_inc(c_nb, 1)

            c_slots(dve, ((4, c_scale), (3, c_statistics), (1, c_add_agg1), (3, c_moments), (1, c_add_agg2)))

        @block.tensor
        def _(pe):
            def transpose_x(g, k, layer, m=P):
                b = g.at % 4
                pe.wait_ge(x_in[b], g.inn(4))
                if g.at > 0:
                    pe.wait_ge(xt_copied, g.times(2, k - 1 + layer))
                for t in range(4):
                    last = nc.tensor.transpose(psum[:, XT[layer][k], t * m:(t + 1) * m],
                                               xg[0:m, b, t, k * P:(k + 1) * P], ident_sb[0:m, 0:m])
                last.then_inc(xt_done, 1)

            def layer1(g, j, m=P):
                pe.wait_ge(xt_split, g.times(2, 2))
                if g.at > 0:
                    pe.wait_ge(h_split, g.times(2, -1 + j))
                cols = slice(j * P, (j + 1) * P)
                nc.tensor.matmul(psum[:, HT[j], 0:4 * m], b1_bf[:, cols], ones3[:, 0:4 * m], start=True, stop=False)
                for k in range(2):
                    for root, part in ((root1_lo, xt_hi), (root1_hi, xt_lo), (root1_hi, xt_hi)):
                        last = nc.tensor.matmul(psum[:, HT[j], 0:4 * m], root[:, k, cols], part[:, k, 0:4 * m],
                                                start=False, stop=(k == 1 and part is xt_hi and root is root1_hi))
                last.then_inc(h_done, 1)

            def layer2(g, q, m=P):
                pe.wait_ge(h_split, g.times(2, 2))
                if g.at > 0 or q > 0:
                    pe.wait_ge(z_added, g.times(2, q))
                nc.tensor.matmul(psum[0:m, ZB, :], ones3[:, 0:m], b2_bf[:, :, :].rearrange("p a d -> p (a d)"),
                                 start=True, stop=False)
                for a in range(2):
                    t = 2 * q + a
                    for j in range(2):
                        for part, root in ((ht_lo, root2_hi), (ht_hi, root2_lo), (ht_hi, root2_hi)):
                            last = nc.tensor.matmul(
                                psum[0:m, ZB, a * D:(a + 1) * D], part[:, j, t * m:(t + 1) * m], root[:, j, :],
                                start=False, stop=(a == 1 and j == 1 and part is ht_hi and root is root2_hi))
                last.then_inc(z_done, 1)

            def slot_weights(e, layer, n):
                if n.at > 0:
                    pe.wait_ge(e.prod, n.n)
                hot = onehot[:, bass.ds(n.n * P, P)]
                for h in range(2):
                    last = nc.tensor.matmul(psum[:, WG + h, :], hot, wcat[:, layer, 512 * h:512 * (h + 1)],
                                            start=True, stop=True)
                last.then_inc(e.wg, 1)

            def transpose_rows(n):
                r = n.at % 4
                pe.wait_ge(eb.x_in[r], n.inn(4))
                if n.at > 0:
                    pe.wait_ge(eb.hpre, n.n)
                for k in range(2):
                    last = nc.tensor.transpose(psum[:, EB, k * P:(k + 1) * P], xe[:, r, k * P:(k + 1) * P],
                                               ident_sb[:, :])
                last.then_inc(eb.xet, 1)

            def source_layer1(n):
                pe.wait_ge(eb.xetc, n.times(1, 1))
                for k in range(2):
                    last = nc.tensor.matmul(XTE, xet[:, n.at % 2, k * P:(k + 1) * P], root1_sb[:, k, :],
                                            start=(k == 0), stop=(k == 1))
                last.then_inc(eb.mm, 1)

            def aggregate(e, n):
                b = n.at % 2
                pe.wait_ge(e.carry, n.times(1, 1))
                pe.wait_ge(e.smat, n.times(1, 1))
                if n.at > 0:
                    pe.wait_ge(e.aggc, n.n)
                nc.tensor.matmul(AGG, smat[:, b, :], msg[:, b, :], start=True, stop=True).then_inc(e.agg, 1)

            def step(e, layer, n, g):
                n2, n3 = n.plus(1), n.plus(2)
                if g is not None:
                    layer2(g, 1, size(g))
                more = g is not None and not past(g.plus(1))
                more2 = g is not None and not past(g.plus(2))
                if more:
                    layer1(g.plus(1), 0, size(g.plus(1)))
                if layer:
                    transpose_rows(n2)
                if more:
                    layer1(g.plus(1), 1, size(g.plus(1)))
                slot_weights(e, layer, n2)
                if layer:
                    source_layer1(n2)
                aggregate(e, n)
                if more2:
                    transpose_x(g.plus(2), 0, layer, size(g.plus(2)))
                if more2 and not layer:
                    transpose_x(g.plus(2), 1, layer, size(g.plus(2)))
                if more:
                    layer2(g.plus(1), 0, size(g.plus(1)))
                if layer and not past_chunks(n3):
                    transpose_rows(n3)
                if more2 and layer:
                    transpose_x(g.plus(2), 1, layer, size(g.plus(2)))
                if not past_chunks(n3):
                    slot_weights(e, layer, n3)
                    if layer:
                        source_layer1(n3)
                aggregate(e, n2)

            pe.wait_ge(descents_ready, 1)
            nc.tensor.matmul(psum[0:1, AG, 0:1], descents[:, :], ones_col[:, :], start=True,
                             stop=True).then_inc(descents_summed, 1)
            pe.wait_ge(ld_const, LD_CONST)
            pe.wait_ge(scan_ready, 1)
            for t, what in enumerate((fwd, bwd)):
                if t:
                    pe.wait_ge(rows_ready, 1)
                for k in range(PIECES):
                    m = min(512, SL - 512 * k)
                    last = nc.tensor.matmul(psum[0:SEG, k, 0:m], sel_sb[:, :], what[:, 512 * k:512 * k + m],
                                            start=True, stop=True)
                last.then_inc(sums_ready, 1)
            pe.wait_ge(ltile_in, 96)
            pe.wait_ge(rows_ready, 2)
            for t in range(2):
                for h, (m, n0) in enumerate(((P, NCH - P), (NCH - P, 0))):
                    last = nc.tensor.transpose(psum[:, t, n0:n0 + m], ltile[0:m, 2 * t + h, :],
                                               anti_sb[0:m, P - m:P])
            last.then_inc(ltr_ready, 1)
            pe.wait_ge(tables_ready, 1)
            pe.wait_ge(onehot_ready, TROWS)
            pe.wait_ge(last_onehot, 1)
            transpose_x(Idx(0), 0, 0)
            transpose_x(Idx(0), 1, 0)
            layer1(Idx(0), 0)
            layer1(Idx(0), 1)
            transpose_x(Idx(1), 0, 0)
            layer2(Idx(0), 0)
            transpose_x(Idx(1), 1, 0)
            slot_weights(ea, 0, Idx(0))
            phase_a(pe, lambda n, g: step(ea, 0, n, g))
            pe.wait_ge(ea.prod, NCH)
            pe.wait_ge(ea.aggc, NCH)
            pe.wait_ge(xt_copied, 2 * (A_G + 2))
            transpose_rows(Idx(0))
            slot_weights(eb, 1, Idx(0))
            source_layer1(Idx(0))
            phase_b(pe, lambda n, g: step(eb, 1, n, g))
            pe.wait_ge(z_added, 2 * (NG + 1))
            pe.wait_ge(eb.aggc, NCH)
            pe.wait_ge(eb.prod, NCH)

            def c_transpose_x(n):
                b, r = n.at % 2, n.at % 4
                pe.wait_ge(c_x_in[r], n.inn(4))
                if n.at >= 2:
                    pe.wait_ge(c_t1c, n.times(1, -1))
                for k in range(2):
                    last = nc.tensor.transpose(psum[:, CT1[b], k * P:(k + 1) * P], xe[:, r, k * P:(k + 1) * P],
                                               ident_sb[:, :])
                last.then_inc(c_t1, 1)

            def c_layer1(n):
                b = n.at % 2
                pe.wait_ge(c_t1c, n.times(1, 1))
                if n.at >= 2:
                    pe.wait_ge(c_hp, n.times(1, -1))
                for k in range(2):
                    last = nc.tensor.matmul(psum[:, CM1[b], 0:D], xet[:, b, k * P:(k + 1) * P], root1_sb[:, k, :],
                                            start=(k == 0), stop=(k == 1))
                last.then_inc(c_m1, 1)

            def c_transpose_h(n):
                b = n.at % 2
                pe.wait_ge(c_h, n.times(1, 1))
                if n.at >= 2:
                    pe.wait_ge(c_t2c, n.times(1, -1))
                for k in range(2):
                    last = nc.tensor.transpose(psum[:, CT2[b], k * P:(k + 1) * P], he[:, b, k * P:(k + 1) * P],
                                               ident_sb[:, :])
                last.then_inc(c_t2, 1)

            def c_layer2(n):
                b = n.at % 2
                pe.wait_ge(c_t2c, n.times(1, 1))
                if n.at >= 2:
                    pe.wait_ge(c_z, n.times(1, -1))
                for k in range(2):
                    last = nc.tensor.matmul(psum[:, CM2[b], 0:D], het[:, b, k * P:(k + 1) * P], root2_sb[:, k, :],
                                            start=(k == 0), stop=(k == 1))
                last.then_inc(c_m2, 1)

            c_slots(pe, ((3, c_layer2), (2, c_transpose_h), (1, c_layer1), (0, c_transpose_x)))


def size(g):
    return RP if g.i is None and g.at == NG else P


def past(g):
    return g.i is None and g.at > NG


def past_chunks(n):
    return n.i is None and n.at >= NCH


def phase_a(eng, step):
    for k in range(PRO // 2):
        step(Idx(2 * k), Idx(k))
    with eng.Fori(0, A_IT) as i:
        for v in range(4):
            step(Idx(PRO + 2 * v, i, 8), Idx(PRO // 2 + v, i))
    for v in range(4):
        step(Idx(NCH - PRO + 2 * v), Idx(A_G - 4 + v))


def phase_b(eng, step):
    for k in range(PRO // 2):
        step(Idx(2 * k), None)
    with eng.Fori(0, B_IT) as i:
        for v in range(4):
            step(Idx(PRO + 2 * v, i, 8), Idx(A_G + v, i))
    for k in range(4):
        step(Idx(NCH - PRO + 2 * k), Idx(NG - 3 + k))


def c_slots(eng, stages):
    lag = max(k for k, _ in stages)
    for n in range(C_PRO):
        for k, stage in stages:
            if n >= k:
                stage(Idx(n - k))
    with eng.Fori(0, C_IT) as i:
        for u in range(4):
            for k, stage in stages:
                stage(Idx(C_PRO + u - k, i))
    for n in range(NCH, NCH + lag):
        for k, stage in stages:
            if n - k < NCH:
                stage(Idx(n - k))


def two(n):
    return n.at // 4 * 32 + 32 if n.i is None else n.i * 32 + (n.at // 4 * 32 + 32)


def kernel(x, src, dst, edge_type_16, L0_gnn_W1, L0_gnn_root1, L0_gnn_bias1, L0_gnn_W2, L0_gnn_root2, L0_gnn_bias2):
    import numpy as np
    import concourse.bacc as bacc
    from concourse.bass_utils import run_bass_kernel_spmd

    def slots(a, fill):
        a = np.asarray(a)
        out = np.full((NCH, P), fill, a.dtype)
        padded = np.full(NCH * EC, fill, a.dtype)
        padded[:E] = a
        out[:, 2:] = padded.reshape(NCH, EC)[::-1]
        return out

    src, dst, typ = (np.asarray(a) for a in (src, dst, edge_type_16))
    around = np.full(E + 2, -1, dst.dtype)
    around[1:-1] = dst
    around[-1] = BIG
    edges = np.zeros((P * EP, 3), dst.dtype)
    edges[:E] = np.stack([dst, typ, src], 1)
    edges[E:, 0] = BIG
    blank = np.zeros((2, NLIN), dst.dtype)
    blank[0] = BIG
    blank[0, 0] = -1
    ar = np.arange(P)
    f = np.float32
    tri = (ar[:, None] >= ar[None, :]).astype(f)
    tri[:, 0] = 1
    tri[0, :] = 1
    tri[:, 1] = 0
    tri[0, 1] = 0
    tri[1, :] = 1
    tri[1, 0] = 0
    iota = np.tile(ar.astype(f), (P, 1))
    iota[:, 0] = 2
    ppos = (ar + 1).astype(f).reshape(P, 1)
    ppos[0] = P + 1
    arrays = dict(
        x=np.asarray(x),
        src=np.ascontiguousarray(slots(src, 0).T), dst=np.ascontiguousarray(slots(dst, BIG).T),
        typ=slots(typ, 0),
        edges=np.ascontiguousarray(edges.reshape(P, EP, 3).transpose(0, 2, 1)),
        eidx=np.arange(P * EP, dtype=f).reshape(P, EP), along=np.arange(SL, dtype=f).reshape(1, SL), blank=blank,
        dstseg=np.stack([around[s * SL:s * SL + SL + 2] for s in range(SEG)]),
        typseg=typ.reshape(SEG, SL),
        w1=np.ascontiguousarray(np.asarray(L0_gnn_W1).transpose(0, 3, 1, 2)).reshape(R, 4 * D),
        w2=np.ascontiguousarray(np.asarray(L0_gnn_W2).transpose(0, 3, 1, 2)).reshape(R, 4 * D),
        root1=np.asarray(L0_gnn_root1), root2=np.asarray(L0_gnn_root2),
        b2=np.stack([np.asarray(L0_gnn_bias1), np.asarray(L0_gnn_bias2)]),
        tri=tri, iota=iota, ppos=ppos,
        rel=np.stack([ar % 16, ar % 32], 1).astype(f),
        sel=(ar[:, None] // 16 == np.arange(SEG)[None, :]).astype(f),
        ident=np.eye(P, dtype=f), anti=np.ascontiguousarray(np.eye(P, dtype=f)[::-1]),
        slotid=np.ascontiguousarray(np.arange(SLOTS, dtype=np.int32).reshape(NCH, P).T),
    )
    nc = bacc.Bacc("TRN2", target_bir_lowering=False, num_devices=1)
    args = {k: nc.dram_tensor(f"in_{k}", a.shape, mybir.dt.from_np(a.dtype), kind="ExternalInput").ap()
            for k, a in arrays.items()}
    y = nc.dram_tensor("out_y", (N, D), F32, kind="ExternalOutput").ap()
    program(nc, **args, y=y)
    r = run_bass_kernel_spmd(nc, [{f"in_{k}": a for k, a in arrays.items()}], core_ids=[0])
    return r.results[0]["out_y"]
```
